# Optimizing a Trainium2 kernel written in Bass

```python
import numpy as np
import jax
import jax.numpy as jnp

def _softmax(x, axis=-1):
    return jax.nn.softmax(x, axis=axis)

def _gelu(x):
    return jax.nn.gelu(x, approximate=True)

def _silu(x):
    return jax.nn.silu(x)

def _sigmoid(x):
    return jax.nn.sigmoid(x)

def _layernorm(x, axis=-1, eps=1e-05):
    m = jnp.mean(x, axis=axis, keepdims=True)
    v = jnp.var(x, axis=axis, keepdims=True)
    return (x - m) / jnp.sqrt(v + eps)

def _scatter_add(tgt, idx, src, axis=0):
    return tgt.at[idx].add(src)

def _segment_sum(src, seg, n):
    return jax.ops.segment_sum(src, seg, n)
kernel_name = 'mk_macaron_d1_jaxref_r8_279c5a'

def setup_inputs(seed: int=0):
    np.random.seed(seed)
    _w = jnp.asarray

    def _L0_attn_setup():
        import jax, jax.numpy as jnp
        import numpy as np
        B, S, D = (1, 512, 128)
        H, KV, WIN = (8, 2, 32)
        HD = D // H
        FP16_MIN = -65504.0
        key = jax.random.key(seed)
        ks = jax.random.split(key, 10)
        sc = 0.02
        return {'x': jax.random.normal(ks[0], (B, S, D), dtype=jnp.float32), 'sink_bias': jnp.float32(0.0), 'Wq': jax.random.normal(ks[1], (H * HD, D), dtype=jnp.float32) * sc, 'bq': jnp.zeros((H * HD,), dtype=jnp.float32), 'Wk': jax.random.normal(ks[2], (KV * HD, D), dtype=jnp.float32) * sc, 'bk': jnp.zeros((KV * HD,), dtype=jnp.float32), 'Wv': jax.random.normal(ks[3], (KV * HD, D), dtype=jnp.float32) * sc, 'bv': jnp.zeros((KV * HD,), dtype=jnp.float32), 'Wo': jax.random.normal(ks[4], (D, H * HD), dtype=jnp.float32) * sc, 'bo': jnp.zeros((D,), dtype=jnp.float32)}
    _L0_attn_in = _L0_attn_setup()

    def _L0_ffn_setup():
        import jax, jax.numpy as jnp
        import numpy as np
        TOP_K = 2
        key = jax.random.key(seed)
        ks = jax.random.split(key, 6)
        B, S, H, F, E = (4, 256, 128, 512, 8)
        x = jax.random.normal(ks[0], (B, S, H), dtype=jnp.float32)
        gate_w = jax.random.normal(ks[1], (E, H), dtype=jnp.float32) * 0.02
        W1 = jax.random.normal(ks[2], (E, H, F), dtype=jnp.float32) * (1.0 / np.sqrt(H))
        b1 = jnp.zeros((E, F), dtype=jnp.float32)
        W2 = jax.random.normal(ks[3], (E, F, H), dtype=jnp.float32) * (1.0 / np.sqrt(F))
        b2 = jnp.zeros((E, H), dtype=jnp.float32)
        sW1 = jax.random.normal(ks[4], (H, F), dtype=jnp.float32) * (1.0 / np.sqrt(H))
        sb1 = jnp.zeros((F,), dtype=jnp.float32)
        sW2 = jax.random.normal(ks[5], (F, H), dtype=jnp.float32) * (1.0 / np.sqrt(F))
        sb2 = jnp.zeros((H,), dtype=jnp.float32)
        return {'x': x, 'gate_w': gate_w, 'W1': W1, 'b1': b1, 'W2': W2, 'b2': b2, 'sW1': sW1, 'sb1': sb1, 'sW2': sW2, 'sb2': sb2}
    _L0_ffn_in = _L0_ffn_setup()
    _d = {'L0_attn_x': _L0_attn_in['x'], 'L0_attn_sink_bias': _L0_attn_in['sink_bias'], 'L0_attn_Wq': _L0_attn_in['Wq'], 'L0_attn_bq': _L0_attn_in['bq'], 'L0_attn_Wk': _L0_attn_in['Wk'], 'L0_attn_bk': _L0_attn_in['bk'], 'L0_attn_Wv': _L0_attn_in['Wv'], 'L0_attn_bv': _L0_attn_in['bv'], 'L0_attn_Wo': _L0_attn_in['Wo'], 'L0_attn_bo': _L0_attn_in['bo'], 'L0_ffn_gate_w': _L0_ffn_in['gate_w'], 'L0_ffn_W1': _L0_ffn_in['W1'], 'L0_ffn_b1': _L0_ffn_in['b1'], 'L0_ffn_W2': _L0_ffn_in['W2'], 'L0_ffn_b2': _L0_ffn_in['b2'], 'L0_ffn_sW1': _L0_ffn_in['sW1'], 'L0_ffn_sb1': _L0_ffn_in['sb1'], 'L0_ffn_sW2': _L0_ffn_in['sW2'], 'L0_ffn_sb2': _L0_ffn_in['sb2']}
    _x0 = _d['L0_attn_x']
    _d['L0_attn_x'] = jax.random.normal(jax.random.fold_in(jax.random.key(seed), 1), (4, 512, 128), dtype=_x0.dtype)
    del _x0
    return _d

def reference(L0_attn_x, L0_attn_sink_bias, L0_attn_Wq, L0_attn_bq, L0_attn_Wk, L0_attn_bk, L0_attn_Wv, L0_attn_bv, L0_attn_Wo, L0_attn_bo, L0_ffn_gate_w, L0_ffn_W1, L0_ffn_b1, L0_ffn_W2, L0_ffn_b2, L0_ffn_sW1, L0_ffn_sb1, L0_ffn_sW2, L0_ffn_sb2):

    def _L0_attn_ref(x, sink_bias, Wq, bq, Wk, bk, Wv, bv, Wo, bo):
        import jax, jax.numpy as jnp
        import numpy as np
        B, S, D = (1, 512, 128)
        H, KV, WIN = (8, 2, 32)
        HD = D // H
        FP16_MIN = -65504.0
        b, s, d = x.shape
        q = (x @ Wq.T + bq).reshape(b, s, H, HD).transpose(0, 2, 1, 3)
        k = (x @ Wk.T + bk).reshape(b, s, KV, HD).transpose(0, 2, 1, 3)
        v = (x @ Wv.T + bv).reshape(b, s, KV, HD).transpose(0, 2, 1, 3)
        k = jnp.repeat(k, H // KV, axis=1)
        v = jnp.repeat(v, H // KV, axis=1)
        scores = jnp.einsum('bhqd,bhkd->bhqk', q, k) / jnp.sqrt(jnp.float32(HD))
        i = jnp.arange(s)[:, None]
        j = jnp.arange(s)[None, :]
        mask = (j <= i) & (j > i - WIN)
        scores = jnp.where(mask, scores, FP16_MIN)
        m = jnp.maximum(scores.max(axis=-1, keepdims=True), sink_bias)
        e = jnp.exp(scores - m)
        sink = jnp.exp(sink_bias - m)
        attn = e / (e.sum(axis=-1, keepdims=True) + sink)
        out = jnp.einsum('bhqk,bhkd->bhqd', attn, v)
        out = out.transpose(0, 2, 1, 3).reshape(b, s, H * HD)
        return out @ Wo.T + bo

    def _L0_ffn_ref(x, gate_w, W1, b1, W2, b2, sW1, sb1, sW2, sb2):
        import jax, jax.numpy as jnp
        import numpy as np
        TOP_K = 2
        B, S, H = x.shape
        E = gate_w.shape[0]
        x_flat = x.reshape(-1, H)
        logits = x_flat @ gate_w.T
        probs = jax.nn.softmax(logits.astype(jnp.float32), axis=-1)
        top_w, sel = jax.lax.top_k(probs, TOP_K)
        top_w = top_w / jnp.sum(top_w, axis=-1, keepdims=True)
        combine = jnp.sum(jax.nn.one_hot(sel, E, dtype=top_w.dtype) * top_w[..., None], axis=1)
        combine = combine.astype(x.dtype)
        h = jax.nn.gelu(jnp.einsum('th,ehf->tef', x_flat, W1) + b1[None], approximate=False)
        y = jnp.einsum('tef,efh->teh', h, W2) + b2[None]
        out = jnp.einsum('teh,te->th', y, combine)
        sh = jax.nn.gelu(x_flat @ sW1 + sb1, approximate=False)
        out = out + sh @ sW2 + sb2
        return out.reshape(B, S, H)
    x = L0_attn_x
    x = x + 0.5 * _L0_ffn_ref(_layernorm(x, axis=-1), L0_ffn_gate_w, L0_ffn_W1, L0_ffn_b1, L0_ffn_W2, L0_ffn_b2, L0_ffn_sW1, L0_ffn_sb1, L0_ffn_sW2, L0_ffn_sb2)
    x = x + _L0_attn_ref(_layernorm(x, axis=-1), L0_attn_sink_bias, L0_attn_Wq, L0_attn_bq, L0_attn_Wk, L0_attn_bk, L0_attn_Wv, L0_attn_bv, L0_attn_Wo, L0_attn_bo)
    x = x + 0.5 * _L0_ffn_ref(_layernorm(x, axis=-1), L0_ffn_gate_w, L0_ffn_W1, L0_ffn_b1, L0_ffn_W2, L0_ffn_b2, L0_ffn_sW1, L0_ffn_sb1, L0_ffn_sW2, L0_ffn_sb2)
    return x

_drawn_inputs = setup_inputs


def setup_inputs(seed=0):
    import zlib

    import numpy as np

    out = dict(_drawn_inputs(seed))
    spreads = {'L0_attn_bq': (0.0, 0.8),
     'L0_attn_bk': (0.0, 0.8),
     'L0_attn_bv': (0.0, 0.1),
     'L0_attn_bo': (0.0, 0.1),
     'L0_ffn_b1': (0.0, 0.1),
     'L0_ffn_b2': (0.0, 0.1),
     'L0_ffn_sb1': (0.0, 0.1),
     'L0_ffn_sb2': (0.0, 0.1)}
    factors = {'L0_attn_Wq': 8.0, 'L0_attn_Wk': 8.0, 'L0_attn_Wv': 2.994}
    for name, (base, spread) in spreads.items():
        noise = np.random.default_rng([zlib.crc32(name.encode()), seed]).standard_normal(out[name].shape)
        drawn = base * np.exp(spread * noise) if base else spread * noise
        out[name] = jnp.asarray(drawn.astype(out[name].dtype))
    for name, factor in factors.items():
        out[name] = (out[name] * factor).astype(out[name].dtype)
    return out
```

```python
from collections import namedtuple
from contextlib import ExitStack

import concourse.bass as bass
from concourse import mybir

ALU = mybir.AluOpType
ACT = mybir.ActivationFunctionType
AX = mybir.AxisListType
F32 = mybir.dt.float32
F16 = mybir.dt.float16
BF16 = mybir.dt.bfloat16

P = 128
WS = 64.0
EPS = 1e-5
MASKED = -1e30

PE_AT = dict(turn_att=11, qk=13, v=14, scores=(18, 27), turn_p=(21, 29), pv=(26, 32), project=35, turn_pre=18,
             logits=23, turn_c=35, logits0=1, turn_c0=5, turn_w=29)
ACT_AT = dict(hi_att=10, q32=14, exp=(20, 29), pt_hi=(23, 29), hi_pre=17, tanh=32, c3t=34, tanh0=2, c3t0=5,
              w_hi=29)
DVE_AT = dict(stats_att=5, var_att=6, xn_att=7, lo_att=10, split_qk=14, mask=15, v=16, max=(17, 27),
              less=(18, 27), pt_lo=(23, 29), norm=(25, 32), turn_o=(27, 33), add=35, stats_pre=9, var_pre=11,
              xn_pre=15, lo_pre=19, router=23, c=33, b2=6, wo=24, w_lo=29)


def macaron_kernel(nc, x_in, sink_in, wq_in, bq_in, wk_in, bk_in, wv_in, bv_in, wo_in, bo_in,
                   gate_in, w1_in, b1_in, w2_in, b2_in, sw1_in, sb1_in, sw2_in, sb2_in, out):
    NBLK, BT, D = x_in.shape
    E, _, F = w1_in.shape
    NE = E + 1
    TT = BT // P
    FC = F // P
    CH = NE * FC
    NU = 2 * NBLK
    KVD = wk_in.shape[0]
    HD = 16
    G = KVD // HD
    HG = D // HD // G
    WIN = 32
    STRIPS = BT // WIN
    HS = STRIPS // 2
    KW = 2 * WIN
    VC = HD + 2
    ZB, HB = 3, 3
    H32 = 4
    assert D == P and CH % ZB == 0 and NE % HB == 0 and CH % H32 == 0

    with ExitStack() as ctx:
        def sb(name, shape, dt=F32):
            return ctx.enter_context(nc.sbuf_tensor(name, shape, dt))

        def sem(name):
            return ctx.enter_context(nc.semaphore(name))

        z = ctx.enter_context(nc.psum_tensor("z", [P, ZB, BT], F32))
        y = ctx.enter_context(nc.psum_tensor("y", [P, 2, BT], F32))
        m = ctx.enter_context(nc.psum_tensor("m", [P, 3, BT], F32))

        x = sb("x", [P, NU, TT, D])
        w1_raw, w2_raw = sb("w1_raw", [P, NE, F]), sb("w2_raw", [P, NE, F])
        w1_hi, w1_lo = sb("w1_hi", [P, NE, FC, P], F16), sb("w1_lo", [P, NE, FC, P], F16)
        w2_hi, w2_lo = sb("w2_hi", [P, NE, FC, D], F16), sb("w2_lo", [P, NE, FC, D], F16)
        b1 = sb("b1", [P, NE, FC])
        xt_hi, xt_lo = sb("xt_hi", [P, NU, BT], F16), sb("xt_lo", [P, NU, BT], F16)
        h32 = sb("h32", [P, H32, BT])
        h_hi, h_lo = sb("h_hi", [P, HB, FC, BT], F16), sb("h_lo", [P, HB, FC, BT], F16)
        ident, ident16, identb = sb("ident", [P, P]), sb("ident16", [P, P], F16), sb("identb", [P, P], BF16)
        gate_raw = sb("gate_raw", [E, D])
        gate_hi, gate_lo = sb("gate_hi", [P, E], F16), sb("gate_lo", [P, E], F16)
        lg, dd, th, sel = (sb(n, [P, TT, E]) for n in ("lg", "dd", "th", "sel"))
        pair, cmp, before = sb("pair", [P, TT, E, E]), sb("cmp", [P, TT, E, E]), sb("before", [P, E, E])
        rank, sl, top = sb("rank", [P, TT, E]), sb("sl", [P, TT, E]), sb("top", [P, TT])
        s_next, s_cur = sb("s_next", [P, TT, E]), sb("s_cur", [P, TT, E])
        c3 = sb("c3", [P, TT, 96], F16)
        c3t = sb("c3t", [96, BT], F16)
        b2_raw, b2_hi = sb("b2_raw", [96, D]), sb("b2_hi", [96, D], F16)
        b2_st = sb("b2_st", [96, D], F16)
        wq_raw, wk_raw, wo_raw = sb("wq_raw", [P, D]), sb("wk_raw", [P, D]), sb("wo_raw", [P, D])
        wo_perm, wv_raw = sb("wo_perm", [P, D]), sb("wv_raw", [KVD, D])
        AW = 3 * P + KVD
        aw_hi, aw_lo = sb("aw_hi", [P, AW], F16), sb("aw_lo", [P, AW], F16)
        bq, bq4, bk = sb("bq", [P, 1]), sb("bq4", [P, 1]), sb("bk", [P, 1])
        bv, bo, sink = sb("bv", [P, KVD]), sb("bo", [P, D]), sb("sink", [P, 1])
        head = sb("head", [P, HG])
        win = sb("win", [P, HS + 1, KW], BF16)
        xa_hi, xa_lo = sb("xa_hi", [P, WIN + BT], F16), sb("xa_lo", [P, WIN + BT], F16)
        xres = sb("xres", [P, TT, D])
        q32, k32 = sb("q32", [P, BT]), sb("k32", [P, BT])
        q_hi, q_lo = sb("q_hi", [P, BT], F16), sb("q_lo", [P, BT], F16)
        k_hi, k_lo = sb("k_hi", [P, WIN + BT], F16), sb("k_lo", [P, WIN + BT], F16)
        qm_hi = sb("qm_hi", [P, STRIPS, HG, WIN], F16)
        qm_lo = sb("qm_lo", [P, STRIPS, HG, WIN], F16)
        v32 = sb("v32", [P, HS, KVD])
        v_hi, v_lo = sb("v_hi", [P, HS, G, VC], F16), sb("v_lo", [P, HS, G, VC], F16)
        NS = G * HS
        mx, mxs = sb("mx", [P, NS]), sb("mxs", [P, NS])
        pe_ = sb("p_exp", [P, NS * KW + NS])
        pt_hi, pt_lo = sb("pt_hi", [P, G, HS // 2, P], F16), sb("pt_lo", [P, G, HS // 2, P], F16)
        den, rden = sb("den", [P, 2, HS // 2, G]), sb("rden", [P, 2, HS // 2, G])
        o32 = sb("o32", [P, HS, G, HD])
        ot32 = sb("ot32", [P, HS * KVD])
        ot_hi, ot_lo = sb("ot_hi", [P, BT], F16), sb("ot_lo", [P, BT], F16)
        half = sb("half", [P, TT])

        Norm = namedtuple("Norm", "stats mv ve rstd xn s_stats s_aggr s_var s_rstd s_xn s_t s_hi s_xt")

        def norm(n):
            return Norm(sb(n + "_stats", [P, TT, 6]), sb(n + "_mv", [P, TT, 2]), sb(n + "_ve", [P, TT]),
                        sb(n + "_rstd", [P, TT]), sb(n + "_xn", [P, TT, D]),
                        sem(n + "_stats_done"), sem(n + "_aggr_done"), sem(n + "_var_ready"),
                        sem(n + "_rstd_ready"), sem(n + "_xn_ready"), sem(n + "_turned"),
                        sem(n + "_hi_ready"), sem(n + "_xt_ready"))

        pre = norm("pre")
        att = norm("att")

        x_loaded = [sem(f"x_loaded{b}") for b in range(NBLK)]
        w1_loaded = [sem(f"w1_loaded{e}") for e in range(NE)]
        w2_loaded = [sem(f"w2_loaded{e}") for e in range(NE)]
        gate_loaded, b1_loaded, b2_loaded = sem("gate_loaded"), sem("b1_loaded"), sem("b2_loaded")
        aw_loaded = sem("aw_loaded")
        made = sem("made")
        dve_made = sem("dve_made")
        gate_turned, gate_hi_done, gate_ready = sem("gate_turned"), sem("gate_hi_done"), sem("gate_ready")
        w1_hi_done, w1_split = sem("w1_hi_done"), sem("w1_split")
        w2_hi_done, w2_split = sem("w2_hi_done"), sem("w2_split")
        b2_step, b2_zero, b2_ready = sem("b2_step"), sem("b2_zero"), sem("b2_ready")
        wo_ready, aw_turned, aw_hi_done, aw_ready = sem("wo_ready"), sem("aw_turned"), sem("aw_hi_done"), sem("aw_ready")
        z_ready = sem("z_ready")
        gelu_done = sem("gelu_done")
        h_hi_done = sem("h_hi_done")
        h_ready = sem("h_ready")
        y_ready = sem("y_ready")
        y_used = sem("y_used")
        lg_ready, gate_step, th_ready = sem("lg_ready"), sem("gate_step"), sem("th_ready")
        c_step = sem("c_step")
        c_ready, c_turned, c_used = sem("c_ready"), sem("c_turned"), sem("c3t_ready")
        s_cur_ready = sem("s_cur_ready")
        qk_done, q32_ready, q_hi_done, q_ready = sem("qk_done"), sem("q32_ready"), sem("q_hi_done"), sem("q_ready")
        q_split = sem("q_split")
        v_done, v32_done, v_hi_done, v_ready = sem("v_done"), sem("v32_done"), sem("v_hi_done"), sem("v_ready")
        s_ready, mx_done, mxs_done, p_ready = sem("s_ready"), sem("mx_done"), sem("mxs_done"), sem("p_ready")
        exp_done, p_turned, pt_hi_done, pt_ready = sem("exp_done"), sem("p_turned"), sem("pt_hi_done"), sem("pt_ready")
        pv_done, den_done, rden_done, o_done = sem("pv_done"), sem("den_done"), sem("rden_done"), sem("o_done")
        ot_turned, ot_hi_done, ot_ready = sem("ot_turned"), sem("ot_hi_done"), sem("ot_ready")
        out_ready, x_attended = sem("out_ready"), sem("x_attended")
        last_tile, stored = sem("last_tile"), sem("stored")

        def slot(buf, u):
            if isinstance(u, int):
                return buf[:, u]
            view = buf[:, bass.ds(u, 1)]
            return view.rearrange("p a t d -> p (a t) d") if len(view.shape) == 4 else view.rearrange("p a t -> p (a t)")

        def wait(eng, s, value):
            if not isinstance(value, int) or value > 0:
                eng.wait_ge(s, value)

        def y_bank(e):
            return y[:, e % 2] if e < NE - 1 else m[:, 0]

        def strided(ap, offset, dims):
            return bass.AP(ap.tensor, offset, dims)

        STEPS = 9

        block = ctx.enter_context(nc.Block())

        @block.sync
        def _(sp):
            def load_x(b):
                sp.dma_start(x[:, b], x_in[b].rearrange("(t p) d -> p t d", p=P)).then_inc(x_loaded[b], 16)

            def load_w1(e):
                src = sw1_in if e == 0 else w1_in[e - 1]
                sp.dma_start(w1_raw[:, e], src).then_inc(w1_loaded[e], 16)

            def load_w2(e):
                src = sw2_in if e == 0 else w2_in[e - 1]
                sp.dma_start(w2_raw[:, e], src.rearrange("(p c) h -> p (c h)", c=FC)).then_inc(w2_loaded[e], 16)

            load_x(0)
            load_w1(0)
            sp.dma_start(b1[:, 0], sb1_in.rearrange("(p c) -> p c", c=FC)).then_inc(b1_loaded, 16)
            sp.dma_start(b1[:, 1:NE], b1_in.rearrange("e (p c) -> p e c", c=FC)).then_inc(b1_loaded, 16)
            load_w2(0)
            for e in range(1, NE):
                load_w1(e)
                load_w2(e)
                if e == 4:
                    load_x(1)
            for b in range(2, NBLK):
                load_x(b)
            with sp.Fori(0, NBLK - 1) as b:
                sp.wait_ge(y_used, b * NE + NE * (NBLK + 1))
                sp.dma_start(out[bass.ds(b, 1)].rearrange("a (t p) d -> p (a t) d", p=P),
                             slot(x, b + NBLK)).then_inc(stored, 16)
            for t in range(TT):
                sp.wait_ge(last_tile, t + 1)
                sp.dma_start(out[NBLK - 1, t * P:(t + 1) * P], x[:, NU - 1, t]).then_inc(stored, 16)
            sp.wait_ge(stored, 16 * (NBLK - 1 + TT))

        @block.gpsimd
        def _(pool):
            pool.dma_start(gate_raw[:, :], gate_in).then_inc(gate_loaded, 16)
            pool.memset(half[:, :], -0.5).then_inc(made, 1)
            pool.memset(ident[:, :], 0.0).then_inc(made, 1)
            pool.wait_ge(made, 2)
            pool.affine_select(out=ident[:, :], in_=ident[:, :], compare_op=ALU.not_equal, fill=1.0,
                               base=0, pattern=[[-1, P]], channel_multiplier=1).then_inc(made, 1)

            def inv_std(n, count):
                pool.wait_ge(n.s_var, count)
                pool.tensor_tensor(n.rstd[:, :], n.ve[:, :], half[:, :], ALU.pow).then_inc(n.s_rstd, 1)

            inv_std(pre, 1)
            pool.memset(before[:, :, :], 0.0).then_inc(made, 1)
            pool.wait_ge(made, 4)
            pool.affine_select(out=before[:, :, :], in_=before[:, :, :], compare_op=ALU.is_gt, fill=1.2e-38,
                               base=0, pattern=[[1, E], [-1, E]], channel_multiplier=0).then_inc(made, 1)
            pool.wait_ge(made, 5)
            pool.affine_select(out=before[:, :, :], in_=before[:, :, :], compare_op=ALU.not_equal, fill=3e38,
                               base=0, pattern=[[1, E], [-1, E]], channel_multiplier=0).then_inc(made, 1)
            pool.wait_ge(b2_zero, 1)
            for p in range(0, 96, 32):
                pool.dma_start(b2_raw[p:p + E, :], b2_in).then_inc(b2_loaded, 16)
                pool.dma_start(b2_raw[p + E:p + E + 1, :], sb2_in.rearrange("(a d) -> a d", a=1)).then_inc(b2_loaded, 16)
            pool.dma_start(wq_raw[:, :], wq_in).then_inc(aw_loaded, 16)
            for g in range(G):
                for h in range(HG):
                    r = (g * HG + h) * HD
                    pool.dma_start(wk_raw[r:r + HD, :], wk_in[g * HD:(g + 1) * HD, :]).then_inc(aw_loaded, 16)
                    pool.dma_start(bk[r:r + HD, :], bk_in[g * HD:(g + 1) * HD].rearrange("(p a) -> p a", a=1))\
                        .then_inc(aw_loaded, 16)
            pool.dma_start(wv_raw[:, :], wv_in).then_inc(aw_loaded, 16)
            pool.dma_start(wo_raw[:, :], wo_in).then_inc(aw_loaded, 16)
            pool.dma_start(bq[:, :], bq_in.rearrange("(p a) -> p a", a=1)).then_inc(aw_loaded, 16)
            pool.dma_start(bv[:, :], strided(bv_in, 0, [[0, P], [1, KVD]])).then_inc(aw_loaded, 16)
            pool.dma_start(bo[:, :], strided(bo_in, 0, [[0, P], [1, D]])).then_inc(aw_loaded, 16)
            pool.dma_start(sink[:, :], strided(sink_in, 0, [[0, P], [1, 1]])).then_inc(aw_loaded, 16)
            pool.memset(head[:, :], 1.0).then_inc(made, 1)
            pool.memset(win[:, :, :], 0.0).then_inc(made, 1)
            for g in range(G):
                rows = head[g * HG * HD:(g + 1) * HG * HD, :]
                pool.wait_ge(made, 8 + 2 * g)
                pool.affine_select(out=rows, in_=rows, compare_op=ALU.is_ge, fill=0.0, base=0,
                                   pattern=[[-HD, HG]], channel_multiplier=1).then_inc(made, 1)
                pool.wait_ge(made, 9 + 2 * g)
                pool.affine_select(out=rows, in_=rows, compare_op=ALU.is_ge, fill=0.0, base=HD - 1,
                                   pattern=[[HD, HG]], channel_multiplier=-1).then_inc(made, 1)
            for h in range(HG):
                rows = win[h * WIN:(h + 1) * WIN]
                pool.wait_ge(made, 12 + 2 * h)
                pool.affine_select(out=rows, in_=rows, compare_op=ALU.is_gt, fill=MASKED, base=0,
                                   pattern=[[0, HS + 1], [1, KW]], channel_multiplier=-1).then_inc(made, 1)
                pool.wait_ge(made, 13 + 2 * h)
                pool.affine_select(out=rows, in_=rows, compare_op=ALU.is_ge, fill=MASKED, base=WIN,
                                   pattern=[[0, HS + 1], [-1, KW]], channel_multiplier=1).then_inc(made, 1)
            pool.wait_ge(made, 20)
            pool.affine_select(out=win[:, 0, :], in_=win[:, 0, :], compare_op=ALU.is_ge, fill=MASKED,
                               base=-WIN, pattern=[[1, KW]], channel_multiplier=0).then_inc(made, 1)
            pool.wait_ge(made, 21)
            inv_std(pre, 2)
            with pool.Fori(1, NBLK + 1) as u:
                inv_std(att, u)
                inv_std(pre, u + 2)
            with pool.Fori(NBLK + 1, NU - 1) as u:
                inv_std(pre, u + 2)

        @block.tensor
        def _(pe):
            def first_product(u, e, c):
                n = 4 * e + c
                if c == 0 and e == 0:
                    pe.wait_ge(pre.s_xt, u + 1)
                if c == 0 and isinstance(u, int) and u == 0:
                    pe.wait_ge(w1_split, e + 1)
                wait(pe, gelu_done, u * CH + n + 1 - ZB)
                bank = z[:, n % ZB, :]
                pe.matmul(bank, w1_hi[:, e, c, :], slot(xt_hi, u), start=True, stop=False)
                pe.matmul(bank, w1_hi[:, e, c, :], slot(xt_lo, u), start=False, stop=False)
                pe.matmul(bank, w1_lo[:, e, c, :], slot(xt_hi, u), start=False, stop=True).then_inc(z_ready, 1)

            def second_product(u, e, c):
                if c == 0:
                    if isinstance(u, int) and u == 0:
                        pe.wait_ge(w2_split, e + 1)
                    wait(pe, y_used, u * NE + e - (2 if e < 2 else 1))
                pe.wait_ge(h_ready, u * CH + 4 * e + c + 1)
                for t in range(TT):
                    cols = slice(t * P, (t + 1) * P)
                    hi, lo, to = h_hi[:, e % HB, c, cols], h_lo[:, e % HB, c, cols], y_bank(e)[:, cols]
                    pe.matmul(to, hi, w2_hi[:, e, c, :], start=(c == 0 and t == 0), stop=False, skip_group_check=True)
                    pe.matmul(to, hi, w2_lo[:, e, c, :], start=False, stop=False, skip_group_check=True)
                    last = pe.matmul(to, lo, w2_hi[:, e, c, :], start=False, stop=(c == FC - 1), skip_group_check=True)
                if e == 0 and c == FC - 1:
                    if isinstance(u, int) and u == 0:
                        pe.wait_ge(b2_ready, 1)
                    pe.wait_ge(c_used, u + 1)
                    for t in range(TT):
                        cols = slice(t * P, (t + 1) * P)
                        last = pe.matmul(y_bank(e)[:, cols], c3t[:, cols], b2_st[:, :], start=False, stop=True,
                                         skip_group_check=True)
                if c == FC - 1:
                    last.then_inc(y_ready, 1)

            def turn(n, count, bank):
                pe.wait_ge(n.s_xn, count)
                for t in range(TT):
                    last = pe.transpose(m[:, bank, t * P:(t + 1) * P], n.xn[:, t, :], ident[:, :])
                last.then_inc(n.s_t, 1)

            def three(to, a_hi, a_lo, b_hi, b_lo, start=True, stop=True):
                pe.matmul(to, a_hi, b_hi, start=start, stop=False, skip_group_check=True)
                pe.matmul(to, a_hi, b_lo, start=False, stop=False, skip_group_check=True)
                return pe.matmul(to, a_lo, b_hi, start=False, stop=stop, skip_group_check=True)

            def logits(v):
                pe.wait_ge(pre.s_xt, v + 1)
                if isinstance(v, int) and v == 0:
                    pe.wait_ge(gate_ready, 1)
                for t in range(TT):
                    cols = slice(t * P, (t + 1) * P)
                    last = three(m[:, 2, t * E:(t + 1) * E], slot(xt_hi, v)[:, cols], slot(xt_lo, v)[:, cols],
                                 gate_hi[:, :], gate_lo[:, :], start=(t == 0))
                last.then_inc(lg_ready, 1)

            def turn_c(v):
                pe.wait_ge(c_ready, v + 1)
                for t in range(TT):
                    last = pe.transpose(m[0:96, 2, t * 64:(t + 1) * 64].bitcast(F16), c3[:, t, :], ident16[:, :])
                last.then_inc(c_turned, 1)

            def turn_weights():
                pe.wait_ge(aw_loaded, 16 * (2 * G * HG + 7))
                pe.transpose(m[:, 0, 0:P], wq_raw[:, :], ident[:, :])
                pe.transpose(m[:, 0, P:2 * P], wk_raw[:, :], ident[:, :])
                pe.wait_ge(wo_ready, 1)
                pe.transpose(m[:, 0, 2 * P:3 * P], wo_perm[:, :], ident[:, :])
                pe.transpose(m[:, 0, 3 * P:AW], wv_raw[:, :], ident[0:KVD, 0:KVD]).then_inc(aw_turned, 1)

            def queries_keys(u):
                pe.wait_ge(att.s_xt, u)
                if isinstance(u, int) is False:
                    pe.wait_ge(aw_ready, 1)
                xh, xl = xa_hi[:, WIN:], xa_lo[:, WIN:]
                three(m[:, 0, :], aw_hi[:, 0:P], aw_lo[:, 0:P], xh, xl)
                three(m[:, 1, :], aw_hi[:, P:2 * P], aw_lo[:, P:2 * P], xh, xl).then_inc(qk_done, 1)

            def values(u):
                for j in range(HS):
                    for par in range(2):
                        at = slice(j * KW + par * WIN, j * KW + par * WIN + KW)
                        last = three(m[par * KW:(par + 1) * KW, 2, j * KVD:(j + 1) * KVD], xa_hi[:, at], xa_lo[:, at],
                                     aw_hi[:, 3 * P:AW], aw_lo[:, 3 * P:AW], start=(j == 0))
                last.then_inc(v_done, 1)

            def scores(u, hf):
                if hf == 0:
                    pe.wait_ge(q_ready, u)
                else:
                    pe.wait_ge(o_done, 2 * u - 1)
                for g in range(G):
                    pe.matmul(m[:, g, :], identb[:, :], win[:, hf:hf + HS, :].rearrange("p s k -> p (s k)"),
                              start=True, stop=False, skip_group_check=True)
                for i in range(HS):
                    s = hf * HS + i
                    for g in range(G):
                        r = slice(g * HG * HD, (g + 1) * HG * HD)
                        last = three(m[:, g, i * KW:(i + 1) * KW],
                                     qm_hi[r, s, :, :].rearrange("p h q -> p (h q)"),
                                     qm_lo[r, s, :, :].rearrange("p h q -> p (h q)"),
                                     k_hi[r, s * WIN:s * WIN + KW], k_lo[r, s * WIN:s * WIN + KW], start=False)
                last.then_inc(s_ready, 1)

            def turn_probs(u, hf):
                pe.wait_ge(exp_done, 2 * u - 1 + hf)
                for g in range(G):
                    for j in range(HS // 2):
                        at = g * HS * KW + j * 2 * KW
                        last = pe.transpose(m[:, g, j * P:(j + 1) * P], pe_[:, at:at + 2 * KW], ident[:, :])
                last.then_inc(p_turned, 1)

            def outputs(u, hf):
                pe.wait_ge(pt_ready, 2 * u - 1 + hf)
                if hf == 0:
                    pe.wait_ge(v_ready, u)
                for j in range(HS // 2):
                    for g in range(G):
                        for par in range(2):
                            r = slice(par * KW, (par + 1) * KW)
                            at = (j * G + g) * VC
                            jj = hf * (HS // 2) + j
                            last = three(m[:, par, at:at + VC], pt_hi[r, g, j, :], pt_lo[r, g, j, :],
                                         v_hi[r, jj, g, :], v_lo[r, jj, g, :], start=(j == 0 and g == 0))
                last.then_inc(pv_done, 1)

            def project(u):
                pe.wait_ge(ot_ready, 2 * u)
                for t in range(TT):
                    cols = slice(t * P, (t + 1) * P)
                    last = three(m[:, 1, cols], ot_hi[:, cols], ot_lo[:, cols],
                                 aw_hi[:, 2 * P:3 * P], aw_lo[:, 2 * P:3 * P], start=(t == 0))
                last.then_inc(out_ready, 1)

            def unit(u, first=False, attend=False, last=False):
                for s in range(NE):
                    for q in range(FC):
                        i = FC * s + q
                        first_product(u, s, q)
                        if s > 0:
                            second_product(u, s - 1, q)
                        elif not first:
                            second_product(u - 1, NE - 1, q)
                        if attend:
                            if i == PE_AT["turn_att"]:
                                turn(att, u, 1)
                            if i == PE_AT["qk"]:
                                queries_keys(u)
                            if i == PE_AT["v"]:
                                values(u)
                            for hf in range(2):
                                if i == PE_AT["scores"][hf]:
                                    scores(u, hf)
                                if i == PE_AT["turn_p"][hf]:
                                    turn_probs(u, hf)
                                if i == PE_AT["pv"][hf]:
                                    outputs(u, hf)
                            if i == PE_AT["project"]:
                                project(u)
                        if not last:
                            if i == PE_AT["turn_pre"]:
                                if attend:
                                    pe.wait_ge(v32_done, u)
                                turn(pre, u + 2, 2)
                            if i == PE_AT["logits"]:
                                logits(u + 1)
                            if i == PE_AT["turn_c"]:
                                turn_c(u + 1)
                        if first:
                            if i == PE_AT["logits0"]:
                                logits(0)
                            if i == PE_AT["turn_c0"]:
                                turn_c(0)
                            if i == PE_AT["turn_w"]:
                                turn_weights()

            pe.wait_ge(made, 3)
            pe.wait_ge(gate_loaded, 16)
            pe.transpose(m[:, 1, 0:E], gate_raw[:, :], ident[0:E, 0:E]).then_inc(gate_turned, 1)
            turn(pre, 1, 2)
            unit(0, first=True)
            with pe.Fori(1, NBLK + 1) as u:
                unit(u, attend=True)
            with pe.Fori(NBLK + 1, NU - 1) as u:
                unit(u)
            unit(NU - 1, last=True)
            for q in range(FC):
                second_product(NU - 1, NE - 1, q)

        @block.scalar
        def _(act):
            def gelu(u, e, c):
                n = 4 * e + c
                act.wait_ge(z_ready, u * CH + n + 1)
                wait(act, h_ready, u * CH + n + 1 - H32)
                bank, bias = z[:, n % ZB, :], b1[:, e, c:c + 1]
                op = act.activation(h32[:, n % H32, :], bank, ACT.Gelu, bias=bias, scale=1 / WS)
                if c < FC - 1:
                    op = act.activation(h_hi[:, e % HB, c, :], bank, ACT.Gelu, bias=bias, scale=1 / WS)
                op.then_inc(gelu_done, 1)

            def split_w1(e):
                act.wait_ge(w1_loaded[e], 16)
                act.activation(w1_hi[:, e], w1_raw[:, e].rearrange("h (p c) -> h c p", c=FC), ACT.Copy, scale=WS)\
                    .then_inc(w1_hi_done, 1)

            def split_w2(e):
                act.wait_ge(w2_loaded[e], 16)
                act.activation(w2_hi[:, e].rearrange("p c h -> p (c h)"), w2_raw[:, e], ACT.Copy, scale=WS)\
                    .then_inc(w2_hi_done, 1)

            def normed_hi(n, count, to, bank):
                act.wait_ge(n.s_t, count)
                act.activation(to, m[:, bank, :], ACT.Copy).then_inc(n.s_hi, 1)

            def tanh(v):
                act.wait_ge(gate_step, v * STEPS + STEPS - 1)
                act.activation(th[:, :, :], dd[:, :, :], ACT.Tanh).then_inc(th_ready, 1)

            def keep_c(v):
                act.wait_ge(c_turned, v + 1)
                act.activation(c3t[:, :], m[0:96, 2, 0:BT // 2].bitcast(F16), ACT.Copy).then_inc(c_used, 1)

            def unit(u, first=False, attend=False, last=False):
                for s in range(NE):
                    for q in range(FC):
                        i = FC * s + q
                        gelu(u, s, q)
                        if attend:
                            if i == ACT_AT["hi_att"]:
                                normed_hi(att, u, xa_hi[:, WIN:], 1)
                            if i == ACT_AT["q32"]:
                                act.wait_ge(qk_done, u)
                                act.activation(q32[:, :], m[:, 0, :], ACT.Identity, bias=bq4[:, :], scale=0.25 / WS)
                                act.activation(k32[:, :], m[:, 1, :], ACT.Identity, bias=bk[:, :], scale=1 / WS)\
                                    .then_inc(q32_ready, 1)
                            for hf in range(2):
                                if i == ACT_AT["exp"][hf]:
                                    act.wait_ge(p_ready, 2 * u - 1 + hf)
                                    act.activation(pe_[:, :], pe_[:, :], ACT.Exp).then_inc(exp_done, 1)
                                if i == ACT_AT["pt_hi"][hf]:
                                    act.wait_ge(p_turned, 2 * u - 1 + hf)
                                    act.activation(pt_hi[:, :, :, :].rearrange("p g j k -> p g (j k)"), m[:, 0:2, :],
                                                   ACT.Copy).then_inc(pt_hi_done, 1)
                        if not last:
                            if i == ACT_AT["hi_pre"]:
                                normed_hi(pre, u + 2, slot(xt_hi, u + 1), 2)
                            if i == ACT_AT["tanh"]:
                                tanh(u + 1)
                            if i == ACT_AT["c3t"]:
                                keep_c(u + 1)
                        if first:
                            if i == 0:
                                split_w2(0)
                            if i == ACT_AT["tanh0"]:
                                tanh(0)
                            if i == ACT_AT["c3t0"]:
                                keep_c(0)
                            if q == 1 and s < NE - 1:
                                split_w1(s + 1)
                            if q == 3 and s < NE - 1:
                                split_w2(s + 1)
                            if i == ACT_AT["w_hi"]:
                                act.wait_ge(aw_turned, 1)
                                act.activation(aw_hi[:, :], m[:, 0, 0:AW], ACT.Copy, scale=WS).then_inc(aw_hi_done, 1)
                                act.activation(bq4[:, :], bq[:, :], ACT.Copy, scale=0.25).then_inc(aw_hi_done, 1)

            split_w1(0)
            act.wait_ge(gate_turned, 1)
            act.activation(gate_hi[:, :], m[:, 1, 0:E], ACT.Copy, scale=WS).then_inc(gate_hi_done, 1)
            normed_hi(pre, 1, slot(xt_hi, 0), 2)
            act.wait_ge(b1_loaded, 32)
            unit(0, first=True)
            act.wait_ge(aw_hi_done, 2)
            with act.Fori(1, NBLK + 1) as u:
                unit(u, attend=True)
            with act.Fori(NBLK + 1, NU - 1) as u:
                unit(u)
            unit(NU - 1, last=True)

        @block.vector
        def _(dve):
            def statistics(n, count, tokens):
                for t in range(TT):
                    op = dve.bn_stats(n.stats[:, t, :], tokens[:, t, :])
                op.then_inc(n.s_stats, 1)

            def variances(n, count):
                for t in range(TT):
                    op = dve.bn_aggr(n.mv[:, t, :], n.stats[:, t, :])
                op.then_inc(n.s_aggr, 1)
                dve.wait_ge(n.s_aggr, count)
                dve.tensor_scalar(n.ve[:, :], n.mv[:, :, 1], EPS, None, ALU.add).then_inc(n.s_var, 1)

            def normalize(n, count, tokens):
                dve.wait_ge(n.s_rstd, count)
                for t in range(TT):
                    op = dve.tensor_scalar(n.xn[:, t, :], tokens[:, t, :], n.mv[:, t, 0:1], n.rstd[:, t:t + 1],
                                           ALU.subtract, ALU.mult)
                op.then_inc(n.s_xn, 1)

            def normed_lo(n, count, to, hi, bank):
                dve.wait_ge(n.s_hi, count)
                dve.tensor_tensor(to, m[:, bank, :], hi, ALU.subtract).then_inc(n.s_xt, 1)

            def hidden(u, e, c):
                n = 4 * e + c
                dve.wait_ge(gelu_done, u * CH + n + 1)
                hi, src = h_hi[:, e % HB, c, :], h32[:, n % H32, :]
                if c == FC - 1:
                    dve.tensor_copy(hi, src).then_inc(h_hi_done, 1)
                    dve.wait_ge(h_hi_done, u * NE + e + 1)
                dve.tensor_tensor(h_lo[:, e % HB, c, :], src, hi, ALU.subtract).then_inc(h_ready, 1)

            def combine(u, e, final=False):
                dve.wait_ge(y_ready, u * NE + e + 1)
                wait(dve, y_used, u * NE + e)
                if e == 1:
                    dve.wait_ge(s_cur_ready, u + 1)
                tokens = slot(x, u)
                for t in range(TT):
                    scale = 0.5 / WS if e == 0 else s_cur[:, t, e - 1:e]
                    op = dve.scalar_tensor_tensor(tokens[:, t, :], y_bank(e)[:, t * P:(t + 1) * P], scale,
                                                  tokens[:, t, :], ALU.mult, ALU.add)
                    if final:
                        op.then_inc(last_tile, 1)
                if not final:
                    op.then_inc(y_used, 1)

            def router(v, step):
                if step > 0:
                    dve.wait_ge(gate_step, v * STEPS + step)
                if step == 0:
                    dve.wait_ge(lg_ready, v + 1)
                    op = dve.tensor_scalar(lg[:, :, :], m[:, 2, 0:TT * E].rearrange("p (t e) -> p t e", e=E),
                                           1 / WS, None, ALU.mult)
                if step == 1:
                    op = dve.tensor_tensor(pair[:, :, :, :], lg[:, :, :].unsqueeze(2).broadcast_to([P, TT, E, E]),
                                           lg[:, :, :].unsqueeze(3).broadcast_to([P, TT, E, E]), ALU.subtract)
                if step == 2:
                    op = dve.tensor_tensor(cmp[:, :, :, :], pair[:, :, :, :],
                                           before[:, :, :].unsqueeze(1).broadcast_to([P, TT, E, E]), ALU.is_ge)
                if step == 3:
                    op = dve.tensor_reduce(rank[:, :, :], cmp[:, :, :, :], AX.X, ALU.add)
                if step == 4:
                    op = dve.tensor_scalar(sel[:, :, :], rank[:, :, :], 1.5, 0.25 / WS, ALU.is_lt, ALU.mult)
                if step == 5:
                    op = dve.tensor_tensor(sl[:, :, :], sel[:, :, :], lg[:, :, :], ALU.mult)
                if step == 6:
                    op = dve.tensor_reduce(top[:, :], sl[:, :, :], AX.X, ALU.add)
                if step == 7:
                    op = dve.scalar_tensor_tensor(dd[:, :, :], top[:, :].unsqueeze(2).broadcast_to([P, TT, E]),
                                                  -2.0 * WS, lg[:, :, :], ALU.mult, ALU.add)
                if step == 8:
                    dve.wait_ge(th_ready, v + 1)
                    op = dve.scalar_tensor_tensor(s_next[:, :, :], th[:, :, :], 1.0, sel[:, :, :], ALU.add, ALU.mult)
                op.then_inc(gate_step, 1)

            def weights_c(v):
                dve.wait_ge(gate_step, v * STEPS + STEPS)
                dve.tensor_scalar(c3[:, :, 0:E], s_next[:, :, :], 2.0 * WS, None, ALU.mult).then_inc(c_step, 1)
                dve.wait_ge(c_step, v + 1)
                dve.scalar_tensor_tensor(c3[:, :, 32:32 + E], s_next[:, :, :], 2.0 * WS, c3[:, :, 0:E],
                                         ALU.mult, ALU.subtract)
                dve.tensor_copy(c3[:, :, 64:64 + E], c3[:, :, 0:E]).then_inc(c_ready, 1)

            def split_w1(e):
                dve.wait_ge(w1_hi_done, e + 1)
                dve.scalar_tensor_tensor(w1_lo[:, e], w1_raw[:, e].rearrange("h (p c) -> h c p", c=FC), WS,
                                         w1_hi[:, e], ALU.mult, ALU.subtract).then_inc(w1_split, 1)

            def split_w2(e):
                dve.wait_ge(w2_hi_done, e + 1)
                dve.scalar_tensor_tensor(w2_lo[:, e].rearrange("p c h -> p (c h)"), w2_raw[:, e], WS,
                                         w2_hi[:, e].rearrange("p c h -> p (c h)"), ALU.mult, ALU.subtract)\
                    .then_inc(w2_split, 1)

            def split_b2():
                dve.wait_ge(b2_loaded, 6 * 16)
                dve.tensor_scalar(b2_hi[:, :], b2_raw[:, :], WS, None, ALU.mult).then_inc(b2_step, 1)
                dve.wait_ge(b2_step, 1)
                dve.tensor_copy(b2_st[0:64, :], b2_hi[0:64, :])
                dve.scalar_tensor_tensor(b2_st[64:96, :], b2_raw[64:96, :], WS, b2_hi[64:96, :],
                                         ALU.mult, ALU.subtract).then_inc(b2_ready, 1)

            def split_qk(u):
                dve.wait_ge(q32_ready, u)
                dve.tensor_copy(q_hi[:, :], q32[:, :])
                dve.tensor_copy(k_hi[:, WIN:], k32[:, :]).then_inc(q_hi_done, 1)
                dve.wait_ge(q_hi_done, u)
                dve.tensor_tensor(q_lo[:, :], q32[:, :], q_hi[:, :], ALU.subtract)
                dve.tensor_tensor(k_lo[:, WIN:], k32[:, :], k_hi[:, WIN:], ALU.subtract).then_inc(q_split, 1)

            def mask_heads(u):
                dve.wait_ge(q_split, u)
                for src, to in ((q_hi, qm_hi), (q_lo, qm_lo)):
                    for h in range(HG):
                        op = dve.tensor_scalar(to[:, :, h, :], src[:, :].rearrange("p (s q) -> p s q", q=WIN),
                                               head[:, h:h + 1], None, ALU.mult)
                op.then_inc(q_ready, 1)

            def keep_values(u):
                dve.wait_ge(v_done, u)
                dve.scalar_tensor_tensor(v32[:, :, :], m[:, 2, 0:HS * KVD].rearrange("p (j c) -> p j c", c=KVD), 1 / WS,
                                         bv[:, :].unsqueeze(1).broadcast_to([P, HS, KVD]), ALU.mult, ALU.add)\
                    .then_inc(v32_done, 1)
                dve.wait_ge(v32_done, u)
                src = v32[:, :, :].rearrange("p j (g d) -> p j g d", d=HD)
                dve.tensor_copy(v_hi[:, :, :, 0:HD], src).then_inc(v_hi_done, 1)
                dve.wait_ge(v_hi_done, u)
                dve.tensor_tensor(v_lo[:, :, :, 0:HD], src, v_hi[:, :, :, 0:HD], ALU.subtract).then_inc(v_ready, 1)

            def softmax_max(u, hf):
                dve.wait_ge(s_ready, 2 * u - 1 + hf)
                dve.tensor_reduce(mx[:, :], m[:, 0:2, :].rearrange("p g (s k) -> p (g s) k", k=KW), AX.X, ALU.max)\
                    .then_inc(mx_done, 1)
                dve.wait_ge(mx_done, 2 * u - 1 + hf)
                dve.tensor_scalar(mxs[:, :], mx[:, :], sink[:, 0:1], None, ALU.max).then_inc(mxs_done, 1)

            def softmax_less_max(u, hf):
                dve.wait_ge(mxs_done, 2 * u - 1 + hf)
                dve.tensor_tensor(pe_[:, 0:NS * KW].rearrange("p (s k) -> p s k", k=KW),
                                  m[:, 0:2, :].rearrange("p g (s k) -> p (g s) k", k=KW),
                                  mxs[:, :].unsqueeze(2).broadcast_to([P, NS, KW]), ALU.subtract)
                dve.tensor_scalar(pe_[:, NS * KW:], mxs[:, :], -1.0, sink[:, 0:1], ALU.mult, ALU.add)\
                    .then_inc(p_ready, 1)

            def probs_lo(u, hf):
                dve.wait_ge(pt_hi_done, 2 * u - 1 + hf)
                dve.tensor_tensor(pt_lo[:, :, :, :].rearrange("p g j k -> p g (j k)"), m[:, 0:2, :],
                                  pt_hi[:, :, :, :].rearrange("p g j k -> p g (j k)"), ALU.subtract)\
                    .then_inc(pt_ready, 1)

            def outputs_norm(u, hf):
                n = 2 * u - 1 + hf
                pv = m[:, 0:2, 0:HS // 2 * G * VC].rearrange("p a (j g c) -> p a j g c", g=G, c=VC)
                dve.wait_ge(pv_done, n)
                dve.tensor_tensor(den[:, :, :, :], pv[:, :, :, :, HD],
                                  pe_[:, NS * KW:].rearrange("p (g j a) -> p a j g", a=2, g=G), ALU.add)\
                    .then_inc(den_done, 1)
                dve.wait_ge(den_done, n)
                dve.reciprocal(rden[:, :, :, :], den[:, :, :, :]).then_inc(rden_done, 1)
                dve.wait_ge(rden_done, n)
                for par in range(2):
                    op = dve.tensor_tensor(o32[:, par::2, :, :], pv[:, par, :, :, 0:HD],
                                           rden[:, par].unsqueeze(3).broadcast_to([P, HS // 2, G, HD]), ALU.mult)
                op.then_inc(o_done, 1)

            def outputs_turn(u, hf):
                n = 2 * u - 1 + hf
                cols = slice(hf * HS * WIN, (hf + 1) * HS * WIN)
                dve.wait_ge(o_done, n)
                dve.transpose(ot32[:, :], o32[:, :, :, :].rearrange("p s g d -> p (s g d)")).then_inc(ot_turned, 1)
                dve.wait_ge(ot_turned, n)
                dve.tensor_copy(ot_hi[:, cols], ot32[:, :]).then_inc(ot_hi_done, 1)
                dve.wait_ge(ot_hi_done, n)
                dve.tensor_tensor(ot_lo[:, cols], ot32[:, :], ot_hi[:, cols], ALU.subtract).then_inc(ot_ready, 1)

            def unit(u, first=False, attend=False, last=False):
                for s in range(NE):
                    for q in range(FC):
                        i = FC * s + q
                        if attend and i == DVE_AT["var_att"]:
                            dve.wait_ge(att.s_stats, u)
                        if not last and i == DVE_AT["var_pre"]:
                            dve.wait_ge(pre.s_stats, u + 2)
                        hidden(u, s, q)
                        if attend and i == DVE_AT["var_att"]:
                            variances(att, u)
                        if not last and i == DVE_AT["var_pre"]:
                            variances(pre, u + 2)
                        if q == 0:
                            if s >= 2:
                                combine(u, s - 2)
                            elif not first:
                                combine(u - 1, NE - 2 + s)
                        if (s, q) == (1, 1):
                            wait(dve, y_used, u * NE)
                            dve.wait_ge(gate_step, (u + 1) * STEPS)
                            dve.tensor_copy(s_cur[:, :, :], s_next[:, :, :]).then_inc(s_cur_ready, 1)
                        if attend:
                            if i == DVE_AT["stats_att"]:
                                dve.wait_ge(y_used, u * NE)
                                dve.tensor_tensor(xres[:, :, :], slot(x, u - 1),
                                                  bo[:, :].unsqueeze(1).broadcast_to([P, TT, D]), ALU.add)
                                statistics(att, u, slot(x, u - 1))
                            if i == DVE_AT["xn_att"]:
                                normalize(att, u, slot(x, u - 1))
                            if i == DVE_AT["lo_att"]:
                                normed_lo(att, u, xa_lo[:, WIN:], xa_hi[:, WIN:], 1)
                            if i == DVE_AT["split_qk"]:
                                split_qk(u)
                            if i == DVE_AT["mask"]:
                                mask_heads(u)
                            if i == DVE_AT["v"]:
                                keep_values(u)
                            for hf in range(2):
                                if i == DVE_AT["max"][hf]:
                                    softmax_max(u, hf)
                                if i == DVE_AT["less"][hf]:
                                    softmax_less_max(u, hf)
                                if i == DVE_AT["pt_lo"][hf]:
                                    probs_lo(u, hf)
                                if i == DVE_AT["norm"][hf]:
                                    outputs_norm(u, hf)
                                if i == DVE_AT["turn_o"][hf]:
                                    outputs_turn(u, hf)
                            if i == DVE_AT["add"]:
                                dve.wait_ge(out_ready, u)
                                dve.scalar_tensor_tensor(slot(x, u + NBLK - 1), m[:, 1, :].rearrange("p (t d) -> p t d", d=D),
                                                         1 / WS, xres[:, :, :], ALU.mult, ALU.add).then_inc(x_attended, 1)
                        if not last:
                            if i == DVE_AT["stats_pre"]:
                                if first:
                                    dve.wait_ge(x_loaded[1], 16)
                                elif attend:
                                    for b in range(2, NBLK):
                                        dve.wait_ge(x_loaded[b], 16)
                                statistics(pre, u + 2, slot(x, u + 1))
                            if i == DVE_AT["xn_pre"]:
                                normalize(pre, u + 2, slot(x, u + 1))
                            if i == DVE_AT["lo_pre"]:
                                normed_lo(pre, u + 2, slot(xt_lo, u + 1), slot(xt_hi, u + 1), 2)
                            for step in range(STEPS):
                                if i == DVE_AT["router"] + step + (step == STEPS - 1):
                                    router(u + 1, step)
                            if i == DVE_AT["c"]:
                                weights_c(u + 1)
                        if first:
                            if (s, q) == (0, 0):
                                split_w2(0)
                                for step in range(0, 3):
                                    router(0, step)
                            if (s, q) == (0, 1):
                                for step in range(3, 8):
                                    router(0, step)
                            if (s, q) == (0, 3):
                                router(0, 8)
                                weights_c(0)
                            if q == 1 and s < NE - 1:
                                split_w1(s + 1)
                            if q == 3 and s < NE - 1:
                                split_w2(s + 1)
                            if i == DVE_AT["b2"]:
                                split_b2()
                            if i == DVE_AT["wo"]:
                                dve.wait_ge(aw_loaded, 16 * (2 * G * HG + 7))
                                dve.tensor_copy(wo_perm[:, :].rearrange("p (h g d) -> p h g d", h=HG, g=G),
                                                wo_raw[:, :].rearrange("p (g h d) -> p h g d", h=HG, g=G))\
                                    .then_inc(wo_ready, 1)
                            if i == DVE_AT["w_lo"]:
                                dve.wait_ge(aw_hi_done, 1)
                                dve.scalar_tensor_tensor(aw_lo[:, :], m[:, 0, 0:AW], WS, aw_hi[:, :], ALU.mult,
                                                         ALU.subtract).then_inc(aw_ready, 1)

            dve.memset(b2_raw[:, :], 0.0).then_inc(b2_zero, 1)
            dve.memset(c3[:, :, :], 0.0).then_inc(dve_made, 1)
            dve.wait_ge(dve_made, 1)
            dve.memset(c3[:, :, E:E + 1], 1.0)
            dve.memset(c3[:, :, 64 + E:65 + E], 1.0)
            dve.memset(xa_hi[:, 0:WIN], 0.0)
            dve.memset(xa_lo[:, 0:WIN], 0.0)
            dve.memset(k_hi[:, 0:WIN], 0.0)
            dve.memset(k_lo[:, 0:WIN], 0.0)
            dve.memset(v_lo[:, :, :, HD:VC], 0.0)
            dve.memset(v_hi[:, :, :, HD:HD + 1], 1.0)
            dve.memset(v_hi[:, :, :, HD + 1:VC], 0.0)
            dve.wait_ge(x_loaded[0], 16)
            statistics(pre, 1, slot(x, 0))
            dve.wait_ge(pre.s_stats, 1)
            variances(pre, 1)
            dve.wait_ge(made, 3)
            dve.tensor_copy(ident16[:, :], ident[:, :])
            dve.tensor_copy(identb[:, :], ident[:, :])
            normalize(pre, 1, slot(x, 0))
            split_w1(0)
            dve.wait_ge(gate_hi_done, 1)
            dve.scalar_tensor_tensor(gate_lo[:, :], m[:, 1, 0:E], WS, gate_hi[:, :], ALU.mult, ALU.subtract)\
                .then_inc(gate_ready, 1)
            normed_lo(pre, 1, slot(xt_lo, 0), slot(xt_hi, 0), 2)
            dve.wait_ge(made, 6)
            unit(0, first=True)
            dve.wait_ge(made, 21)
            with dve.Fori(1, NBLK + 1) as u:
                unit(u, attend=True)
            with dve.Fori(NBLK + 1, NU - 1) as u:
                unit(u)
            unit(NU - 1, last=True)
            combine(NU - 1, NE - 2)
            combine(NU - 1, NE - 1, final=True)


_INS = ["L0_attn_x", "L0_attn_sink_bias", "L0_attn_Wq", "L0_attn_bq", "L0_attn_Wk", "L0_attn_bk", "L0_attn_Wv",
        "L0_attn_bv", "L0_attn_Wo", "L0_attn_bo", "L0_ffn_gate_w", "L0_ffn_W1", "L0_ffn_b1", "L0_ffn_W2",
        "L0_ffn_b2", "L0_ffn_sW1", "L0_ffn_sb1", "L0_ffn_sW2", "L0_ffn_sb2"]
_OUTS = [((4, 512, 128), "float32")]


def kernel(**inputs):
    import numpy as _np
    import concourse.bacc as _bacc
    from concourse import mybir as _mybir
    from concourse.bass_utils import run_bass_kernel_spmd as _run

    nc = _bacc.Bacc("TRN2", target_bir_lowering=False, num_devices=1)
    arrays, args = {}, []
    for name in _INS:
        a = _np.ascontiguousarray(inputs[name])
        arrays[f"in_{name}_dram"] = a
        args.append(nc.dram_tensor(f"in_{name}_dram", a.shape, _mybir.dt.from_np(a.dtype), kind="ExternalInput").ap())
    for i, (shape, dtype) in enumerate(_OUTS):
        dt = _mybir.dt.from_np(_np.dtype(dtype))
        args.append(nc.dram_tensor(f"out_{i}_dram", shape, dt, kind="ExternalOutput").ap())
    macaron_kernel(nc, *args)
    r = _run(nc, [arrays], core_ids=[0])
    return r.results[0]["out_0_dram"]
```

```python
from collections import namedtuple
from contextlib import ExitStack

import concourse.bass as bass
from concourse import mybir

ALU = mybir.AluOpType
ACT = mybir.ActivationFunctionType
AX = mybir.AxisListType
F32 = mybir.dt.float32
F16 = mybir.dt.float16
BF16 = mybir.dt.bfloat16

P = 128
WS = 64.0
EPS = 1e-5
MASKED = -1e30

PE_AT = dict(turn_att=12, qk=14, v=15, scores=(23, 5), turn_p=(29, 11), pv=(34, 13), project=21, turn_pre=23,
             logits=25, turn_c=9, logits0=1, turn_w=28)
ACT_AT = dict(hi_att=12, q32=15, exp=(27, 8), pt_hi=(29, 10), hi_pre=23, tanh=34, c3t=9, tanh0=6, w_hi=29)
DVE_AT = dict(stats_att=5, var_att=8, xn_att=8, lo_att=11, split_qk=15, v=16, max=(23, 5), less=(24, 7),
              pt_lo=(29, 10), norm=(32, 11), turn_o=(33, 14), xres=7, add=20, stats_pre=8, var_pre=10, xn_pre=19,
              lo_pre=23, router=25, s_cur=5, c=5, router0=2, b2=20, wo=23, w_lo=32)


def macaron_kernel(nc, x_in, sink_in, wq_in, bq_in, wk_in, bk_in, wv_in, bv_in, wo_in, bo_in,
                   gate_in, w1_in, b1_in, w2_in, b2_in, sw1_in, sb1_in, sw2_in, sb2_in, out):
    NBLK, BT, D = x_in.shape
    E, _, F = w1_in.shape
    NE = E + 1
    SHARED = E
    TT = BT // P
    FC = F // P
    CH = NE * FC
    NU = 2 * NBLK
    KVD = wk_in.shape[0]
    HD = 16
    G = KVD // HD
    HG = D // HD // G
    WIN = 32
    STRIPS = BT // WIN
    HS = STRIPS // 2
    KW = 2 * WIN
    VC = HD + 2
    ZB, HB = 3, 3
    H32 = 4
    assert D == P and CH % ZB == 0 and NE % HB == 0 and CH % H32 == 0

    with ExitStack() as ctx:
        def sb(name, shape, dt=F32):
            return ctx.enter_context(nc.sbuf_tensor(name, shape, dt))

        def sem(name):
            return ctx.enter_context(nc.semaphore(name))

        z = ctx.enter_context(nc.psum_tensor("z", [P, ZB, BT], F32))
        y = ctx.enter_context(nc.psum_tensor("y", [P, 2, BT], F32))
        m = ctx.enter_context(nc.psum_tensor("m", [P, 3, BT], F32))

        x = sb("x", [P, NU, TT, D])
        w1_raw, w2_raw = sb("w1_raw", [P, NE, F]), sb("w2_raw", [P, NE, F])
        w1_hi, w1_lo = sb("w1_hi", [P, NE, FC, P], F16), sb("w1_lo", [P, NE, FC, P], F16)
        w2_hi, w2_lo = sb("w2_hi", [P, NE, FC, D], F16), sb("w2_lo", [P, NE, FC, D], F16)
        b1 = sb("b1", [P, NE, FC])
        xt_hi, xt_lo = sb("xt_hi", [P, NU, BT], F16), sb("xt_lo", [P, NU, BT], F16)
        h32 = sb("h32", [P, H32, BT])
        h_hi, h_lo = sb("h_hi", [P, HB, FC, BT], F16), sb("h_lo", [P, HB, FC, BT], F16)
        ident, ident16, identb = sb("ident", [P, P]), sb("ident16", [P, P], F16), sb("identb", [P, P], BF16)
        gate_raw = sb("gate_raw", [E, D])
        gate_hi, gate_lo = sb("gate_hi", [P, E], F16), sb("gate_lo", [P, E], F16)
        lg, dd, th, sel = (sb(n, [P, TT, E]) for n in ("lg", "dd", "th", "sel"))
        pair, cmp, before = sb("pair", [P, TT, E, E]), sb("cmp", [P, TT, E, E]), sb("before", [P, E, E])
        rank, sl, top = sb("rank", [P, TT, E]), sb("sl", [P, TT, E]), sb("top", [P, TT])
        s_next, s_cur = sb("s_next", [P, TT, E]), sb("s_cur", [P, TT, E])
        c3 = sb("c3", [P, TT, 96], F16)
        c3t = sb("c3t", [96, BT], F16)
        b2_raw, b2_hi = sb("b2_raw", [96, D]), sb("b2_hi", [96, D], F16)
        b2_st = sb("b2_st", [96, D], F16)
        wq_raw, wk_raw, wo_raw = sb("wq_raw", [P, D]), sb("wk_raw", [P, D]), sb("wo_raw", [P, D])
        wo_perm, wv_raw = sb("wo_perm", [P, D]), sb("wv_raw", [KVD, D])
        AW = 3 * P + KVD
        aw_hi, aw_lo = sb("aw_hi", [P, AW], F16), sb("aw_lo", [P, AW], F16)
        bq, bq4, bk = sb("bq", [P, 1]), sb("bq4", [P, 1]), sb("bk", [P, 1])
        bv, bo, sink = sb("bv", [P, KVD]), sb("bo", [P, D]), sb("sink", [P, 1])
        head = sb("head", [P, HG])
        win = sb("win", [P, HS + 1, KW], BF16)
        xa_hi, xa_lo = sb("xa_hi", [P, WIN + BT], F16), sb("xa_lo", [P, WIN + BT], F16)
        xres = sb("xres", [P, TT, D])
        q32, k32 = sb("q32", [P, BT]), sb("k32", [P, BT])
        q_hi, q_lo = sb("q_hi", [P, BT], F16), sb("q_lo", [P, BT], F16)
        k_hi, k_lo = sb("k_hi", [P, WIN + BT], F16), sb("k_lo", [P, WIN + BT], F16)
        qm_hi = sb("qm_hi", [P, STRIPS, HG, WIN], F16)
        qm_lo = sb("qm_lo", [P, STRIPS, HG, WIN], F16)
        v32 = sb("v32", [P, HS, KVD])
        v_hi, v_lo = sb("v_hi", [P, HS, G, VC], F16), sb("v_lo", [P, HS, G, VC], F16)
        NS = G * HS
        mx, mxs = sb("mx", [P, NS]), sb("mxs", [P, NS])
        pe_ = sb("p_exp", [P, NS * KW + NS])
        pt_hi, pt_lo = sb("pt_hi", [P, G, HS // 2, P], F16), sb("pt_lo", [P, G, HS // 2, P], F16)
        den, rden = sb("den", [P, 2, HS // 2, G]), sb("rden", [P, 2, HS // 2, G])
        o32 = sb("o32", [P, HS, G, HD])
        ot32 = sb("ot32", [P, HS * KVD])
        ot_hi, ot_lo = sb("ot_hi", [P, BT], F16), sb("ot_lo", [P, BT], F16)
        half = sb("half", [P, TT])

        Norm = namedtuple("Norm", "stats mv ve rstd xn s_stats s_aggr s_var s_rstd s_xn s_t s_hi s_xt")

        def norm(n):
            return Norm(sb(n + "_stats", [P, TT, 6]), sb(n + "_mv", [P, TT, 2]), sb(n + "_ve", [P, TT]),
                        sb(n + "_rstd", [P, TT]), sb(n + "_xn", [P, TT, D]),
                        sem(n + "_stats_done"), sem(n + "_aggr_done"), sem(n + "_var_ready"),
                        sem(n + "_rstd_ready"), sem(n + "_xn_ready"), sem(n + "_turned"),
                        sem(n + "_hi_ready"), sem(n + "_xt_ready"))

        pre = norm("pre")
        att = norm("att")

        x_loaded = [sem(f"x_loaded{b}") for b in range(NBLK)]
        w1_loaded = [sem(f"w1_loaded{e}") for e in range(NE)]
        w2_loaded = [sem(f"w2_loaded{e}") for e in range(NE)]
        gate_loaded, b1_loaded, b2_loaded = sem("gate_loaded"), sem("b1_loaded"), sem("b2_loaded")
        aw_loaded = sem("aw_loaded")
        made = sem("made")
        dve_made = sem("dve_made")
        gate_turned, gate_hi_done, gate_ready = sem("gate_turned"), sem("gate_hi_done"), sem("gate_ready")
        w1_hi_done, w1_split = sem("w1_hi_done"), sem("w1_split")
        w2_hi_done, w2_split = sem("w2_hi_done"), sem("w2_split")
        b2_step, b2_zero, b2_ready = sem("b2_step"), sem("b2_zero"), sem("b2_ready")
        wo_ready, aw_turned, aw_hi_done, aw_ready = sem("wo_ready"), sem("aw_turned"), sem("aw_hi_done"), sem("aw_ready")
        z_ready = sem("z_ready")
        gelu_done = sem("gelu_done")
        h_hi_done = sem("h_hi_done")
        h_ready = sem("h_ready")
        y_ready = sem("y_ready")
        y_used = sem("y_used")
        lg_ready, gate_step, th_ready = sem("lg_ready"), sem("gate_step"), sem("th_ready")
        c_step = sem("c_step")
        c_ready, c_turned, c_used = sem("c_ready"), sem("c_turned"), sem("c3t_ready")
        s_cur_ready = sem("s_cur_ready")
        qk_done, q32_ready, q_hi_done, q_ready = sem("qk_done"), sem("q32_ready"), sem("q_hi_done"), sem("q_ready")
        q_split = sem("q_split")
        v_done, v32_done, v_hi_done, v_ready = sem("v_done"), sem("v32_done"), sem("v_hi_done"), sem("v_ready")
        s_ready, mx_done, mxs_done, p_ready = sem("s_ready"), sem("mx_done"), sem("mxs_done"), sem("p_ready")
        exp_done, p_turned, pt_hi_done, pt_ready = sem("exp_done"), sem("p_turned"), sem("pt_hi_done"), sem("pt_ready")
        pv_done, den_done, rden_done, o_done = sem("pv_done"), sem("den_done"), sem("rden_done"), sem("o_done")
        ot_turned, ot_hi_done, ot_ready = sem("ot_turned"), sem("ot_hi_done"), sem("ot_ready")
        out_ready, xres_done, x_attended = sem("out_ready"), sem("xres_done"), sem("x_attended")
        last_tile, stored = sem("last_tile"), sem("stored")

        def slot(buf, u):
            if isinstance(u, int):
                return buf[:, u]
            view = buf[:, bass.ds(u, 1)]
            return view.rearrange("p a t d -> p (a t) d") if len(view.shape) == 4 else view.rearrange("p a t -> p (a t)")

        def wait(eng, s, value):
            if not isinstance(value, int) or value > 0:
                eng.wait_ge(s, value)

        def nth_half(u, hf):
            return 2 * u - 1 if hf == 0 else 2 * u - 2

        def y_bank(e):
            return y[:, e % 2] if e != SHARED else m[:, 2]

        def strided(ap, offset, dims):
            return bass.AP(ap.tensor, offset, dims)

        STEPS = 9

        block = ctx.enter_context(nc.Block())

        @block.sync
        def _(sp):
            def load_x(b):
                sp.dma_start(x[:, b], x_in[b].rearrange("(t p) d -> p t d", p=P)).then_inc(x_loaded[b], 16)

            def load_w1(e):
                src = sw1_in if e == SHARED else w1_in[e]
                sp.dma_start(w1_raw[:, e], src).then_inc(w1_loaded[e], 16)

            def load_w2(e):
                src = sw2_in if e == SHARED else w2_in[e]
                sp.dma_start(w2_raw[:, e], src.rearrange("(p c) h -> p (c h)", c=FC)).then_inc(w2_loaded[e], 16)

            load_x(0)
            load_w1(0)
            sp.dma_start(b1[:, 0:E], b1_in.rearrange("e (p c) -> p e c", c=FC)).then_inc(b1_loaded, 16)
            sp.dma_start(b1[:, SHARED], sb1_in.rearrange("(p c) -> p c", c=FC)).then_inc(b1_loaded, 16)
            load_w2(0)
            for e in range(1, NE):
                load_w1(e)
                load_w2(e)
                if e == 4:
                    load_x(1)
            for b in range(2, NBLK):
                load_x(b)
            with sp.Fori(0, NBLK - 1) as b:
                sp.wait_ge(y_used, b * NE + NE * (NBLK + 1))
                sp.dma_start(out[bass.ds(b, 1)].rearrange("a (t p) d -> p (a t) d", p=P),
                             slot(x, b + NBLK)).then_inc(stored, 16)
            for t in range(TT):
                sp.wait_ge(last_tile, t + 1)
                sp.dma_start(out[NBLK - 1, t * P:(t + 1) * P], x[:, NU - 1, t]).then_inc(stored, 16)
            sp.wait_ge(stored, 16 * (NBLK - 1 + TT))

        @block.gpsimd
        def _(pool):
            pool.dma_start(gate_raw[:, :], gate_in).then_inc(gate_loaded, 16)
            pool.memset(half[:, :], -0.5).then_inc(made, 1)
            pool.memset(ident[:, :], 0.0).then_inc(made, 1)
            pool.wait_ge(made, 2)
            pool.affine_select(out=ident[:, :], in_=ident[:, :], compare_op=ALU.not_equal, fill=1.0,
                               base=0, pattern=[[-1, P]], channel_multiplier=1).then_inc(made, 1)

            def inv_std(n, count):
                pool.wait_ge(n.s_var, count)
                pool.tensor_tensor(n.rstd[:, :], n.ve[:, :], half[:, :], ALU.pow).then_inc(n.s_rstd, 1)

            def mask_heads(u, hf):
                pool.wait_ge(q_split, u)
                strips = slice(hf * HS, (hf + 1) * HS)
                for src, to in ((q_hi, qm_hi), (q_lo, qm_lo)):
                    queries = src[:, :].rearrange("p (s q) -> p s q", q=WIN)[:, strips]
                    pool.tensor_tensor(to[:, strips, 0, :], queries, head[:, 0:1].unsqueeze(2).broadcast_to([P, HS, WIN]),
                                       ALU.mult)
                    for h in range(1, HG):
                        op = pool.tensor_scalar(to[:, strips, h, :], queries, head[:, h:h + 1], None, ALU.mult)
                op.then_inc(q_ready, 1)

            inv_std(pre, 1)
            pool.memset(before[:, :, :], 0.0).then_inc(made, 1)
            pool.wait_ge(made, 4)
            pool.affine_select(out=before[:, :, :], in_=before[:, :, :], compare_op=ALU.is_gt, fill=1.2e-38,
                               base=0, pattern=[[1, E], [-1, E]], channel_multiplier=0).then_inc(made, 1)
            pool.wait_ge(made, 5)
            pool.affine_select(out=before[:, :, :], in_=before[:, :, :], compare_op=ALU.not_equal, fill=3e38,
                               base=0, pattern=[[1, E], [-1, E]], channel_multiplier=0).then_inc(made, 1)
            pool.wait_ge(b2_zero, 1)
            for p in range(0, 96, 32):
                pool.dma_start(b2_raw[p:p + E, :], b2_in).then_inc(b2_loaded, 16)
                pool.dma_start(b2_raw[p + E:p + E + 1, :], sb2_in.rearrange("(a d) -> a d", a=1)).then_inc(b2_loaded, 16)
            pool.dma_start(wq_raw[:, :], wq_in).then_inc(aw_loaded, 16)
            for g in range(G):
                for h in range(HG):
                    r = (g * HG + h) * HD
                    pool.dma_start(wk_raw[r:r + HD, :], wk_in[g * HD:(g + 1) * HD, :]).then_inc(aw_loaded, 16)
                    pool.dma_start(bk[r:r + HD, :], bk_in[g * HD:(g + 1) * HD].rearrange("(p a) -> p a", a=1))\
                        .then_inc(aw_loaded, 16)
            pool.dma_start(wv_raw[:, :], wv_in).then_inc(aw_loaded, 16)
            pool.dma_start(wo_raw[:, :], wo_in).then_inc(aw_loaded, 16)
            pool.dma_start(bq[:, :], bq_in.rearrange("(p a) -> p a", a=1)).then_inc(aw_loaded, 16)
            pool.dma_start(bv[:, :], strided(bv_in, 0, [[0, P], [1, KVD]])).then_inc(aw_loaded, 16)
            pool.dma_start(bo[:, :], strided(bo_in, 0, [[0, P], [1, D]])).then_inc(aw_loaded, 16)
            pool.dma_start(sink[:, :], strided(sink_in, 0, [[0, P], [1, 1]])).then_inc(aw_loaded, 16)
            pool.memset(head[:, :], 1.0).then_inc(made, 1)
            pool.memset(win[:, :, :], 0.0).then_inc(made, 1)
            for g in range(G):
                rows = head[g * HG * HD:(g + 1) * HG * HD, :]
                pool.wait_ge(made, 8 + 2 * g)
                pool.affine_select(out=rows, in_=rows, compare_op=ALU.is_ge, fill=0.0, base=0,
                                   pattern=[[-HD, HG]], channel_multiplier=1).then_inc(made, 1)
                pool.wait_ge(made, 9 + 2 * g)
                pool.affine_select(out=rows, in_=rows, compare_op=ALU.is_ge, fill=0.0, base=HD - 1,
                                   pattern=[[HD, HG]], channel_multiplier=-1).then_inc(made, 1)
            for h in range(HG):
                rows = win[h * WIN:(h + 1) * WIN]
                pool.wait_ge(made, 12 + 2 * h)
                pool.affine_select(out=rows, in_=rows, compare_op=ALU.is_gt, fill=MASKED, base=0,
                                   pattern=[[0, HS + 1], [1, KW]], channel_multiplier=-1).then_inc(made, 1)
                pool.wait_ge(made, 13 + 2 * h)
                pool.affine_select(out=rows, in_=rows, compare_op=ALU.is_ge, fill=MASKED, base=WIN,
                                   pattern=[[0, HS + 1], [-1, KW]], channel_multiplier=1).then_inc(made, 1)
            pool.wait_ge(made, 20)
            pool.affine_select(out=win[:, 0, :], in_=win[:, 0, :], compare_op=ALU.is_ge, fill=MASKED,
                               base=-WIN, pattern=[[1, KW]], channel_multiplier=0).then_inc(made, 1)
            pool.wait_ge(made, 21)
            inv_std(pre, 2)
            with pool.Fori(1, NBLK + 1) as u:
                inv_std(att, u)
                inv_std(pre, u + 2)
                mask_heads(u, 0)
                mask_heads(u, 1)
            with pool.Fori(NBLK + 1, NU - 1) as u:
                inv_std(pre, u + 2)

        @block.tensor
        def _(pe):
            def first_product(u, e, c):
                n = 4 * e + c
                if c == 0 and e == 0:
                    pe.wait_ge(pre.s_xt, u + 1)
                if c == 0 and isinstance(u, int) and u == 0:
                    pe.wait_ge(w1_split, e + 1)
                wait(pe, gelu_done, u * CH + n + 1 - ZB)
                bank = z[:, n % ZB, :]
                pe.matmul(bank, w1_hi[:, e, c, :], slot(xt_hi, u), start=True, stop=False)
                pe.matmul(bank, w1_hi[:, e, c, :], slot(xt_lo, u), start=False, stop=False)
                pe.matmul(bank, w1_lo[:, e, c, :], slot(xt_hi, u), start=False, stop=True).then_inc(z_ready, 1)

            def second_product(u, e, c):
                if c == 0:
                    if isinstance(u, int) and u == 0:
                        pe.wait_ge(w2_split, e + 1)
                    wait(pe, y_used, u * NE + e - (2 if e < 2 else 1))
                    if e == SHARED and not (isinstance(u, int) and u == NU - 1):
                        pe.wait_ge(gate_step, (u + 1) * STEPS + 1)
                pe.wait_ge(h_ready, u * CH + 4 * e + c + 1)
                for t in range(TT):
                    cols = slice(t * P, (t + 1) * P)
                    hi, lo, to = h_hi[:, e % HB, c, cols], h_lo[:, e % HB, c, cols], y_bank(e)[:, cols]
                    pe.matmul(to, hi, w2_hi[:, e, c, :], start=(c == 0 and t == 0), stop=False, skip_group_check=True)
                    pe.matmul(to, hi, w2_lo[:, e, c, :], start=False, stop=False, skip_group_check=True)
                    last = pe.matmul(to, lo, w2_hi[:, e, c, :], start=False, stop=(c == FC - 1), skip_group_check=True)
                if e == SHARED and c == FC - 1:
                    if isinstance(u, int) and u == 0:
                        pe.wait_ge(b2_ready, 1)
                    pe.wait_ge(c_used, u + 1)
                    for t in range(TT):
                        cols = slice(t * P, (t + 1) * P)
                        last = pe.matmul(y_bank(e)[:, cols], c3t[:, cols], b2_st[:, :], start=False, stop=True,
                                         skip_group_check=True)
                if c == FC - 1:
                    last.then_inc(y_ready, 1)

            def turn(n, count, bank):
                pe.wait_ge(n.s_xn, count)
                for t in range(TT):
                    last = pe.transpose(m[:, bank, t * P:(t + 1) * P], n.xn[:, t, :], ident[:, :])
                last.then_inc(n.s_t, 1)

            def three(to, a_hi, a_lo, b_hi, b_lo, start=True, stop=True):
                pe.matmul(to, a_hi, b_hi, start=start, stop=False, skip_group_check=True)
                pe.matmul(to, a_hi, b_lo, start=False, stop=False, skip_group_check=True)
                return pe.matmul(to, a_lo, b_hi, start=False, stop=stop, skip_group_check=True)

            def logits(v):
                pe.wait_ge(pre.s_xt, v + 1)
                if isinstance(v, int) and v == 0:
                    pe.wait_ge(gate_ready, 1)
                for t in range(TT):
                    cols = slice(t * P, (t + 1) * P)
                    last = three(m[:, 2, t * E:(t + 1) * E], slot(xt_hi, v)[:, cols], slot(xt_lo, v)[:, cols],
                                 gate_hi[:, :], gate_lo[:, :], start=(t == 0))
                last.then_inc(lg_ready, 1)

            def turn_c(v):
                wait(pe, y_used, v * NE)
                pe.wait_ge(c_ready, v + 1)
                for t in range(TT):
                    last = pe.transpose(m[0:96, 2, t * 64:(t + 1) * 64].bitcast(F16), c3[:, t, :], ident16[:, :])
                last.then_inc(c_turned, 1)

            def turn_weights():
                pe.wait_ge(aw_loaded, 16 * (2 * G * HG + 7))
                pe.transpose(m[:, 0, 0:P], wq_raw[:, :], ident[:, :])
                pe.transpose(m[:, 0, P:2 * P], wk_raw[:, :], ident[:, :])
                pe.wait_ge(wo_ready, 1)
                pe.transpose(m[:, 0, 2 * P:3 * P], wo_perm[:, :], ident[:, :])
                pe.transpose(m[:, 0, 3 * P:AW], wv_raw[:, :], ident[0:KVD, 0:KVD]).then_inc(aw_turned, 1)

            def queries_keys(u):
                pe.wait_ge(att.s_xt, u)
                if isinstance(u, int):
                    pe.wait_ge(aw_ready, 1)
                xh, xl = xa_hi[:, WIN:], xa_lo[:, WIN:]
                three(m[:, 0, :], aw_hi[:, 0:P], aw_lo[:, 0:P], xh, xl)
                three(m[:, 1, :], aw_hi[:, P:2 * P], aw_lo[:, P:2 * P], xh, xl).then_inc(qk_done, 1)

            def values(u):
                pe.wait_ge(att.s_xt, u)
                if isinstance(u, int):
                    pe.wait_ge(aw_ready, 1)
                for j in range(HS):
                    for par in range(2):
                        at = slice(j * KW + par * WIN, j * KW + par * WIN + KW)
                        last = three(m[par * KW:(par + 1) * KW, 2, j * KVD:(j + 1) * KVD], xa_hi[:, at], xa_lo[:, at],
                                     aw_hi[:, 3 * P:AW], aw_lo[:, 3 * P:AW], start=(j == 0))
                last.then_inc(v_done, 1)

            def scores(u, hf):
                pe.wait_ge(q_ready, nth_half(u, hf))
                if hf == 1:
                    pe.wait_ge(o_done, nth_half(u, 1) - 1)
                for g in range(G):
                    pe.matmul(m[:, g, :], identb[:, :], win[:, hf:hf + HS, :].rearrange("p s k -> p (s k)"),
                              start=True, stop=False, skip_group_check=True)
                for i in range(HS):
                    s = hf * HS + i
                    for g in range(G):
                        r = slice(g * HG * HD, (g + 1) * HG * HD)
                        last = three(m[:, g, i * KW:(i + 1) * KW],
                                     qm_hi[r, s, :, :].rearrange("p h q -> p (h q)"),
                                     qm_lo[r, s, :, :].rearrange("p h q -> p (h q)"),
                                     k_hi[r, s * WIN:s * WIN + KW], k_lo[r, s * WIN:s * WIN + KW], start=False)
                last.then_inc(s_ready, 1)

            def turn_probs(u, hf):
                pe.wait_ge(exp_done, nth_half(u, hf))
                for g in range(G):
                    for j in range(HS // 2):
                        at = g * HS * KW + j * 2 * KW
                        last = pe.transpose(m[:, g, j * P:(j + 1) * P], pe_[:, at:at + 2 * KW], ident[:, :])
                last.then_inc(p_turned, 1)

            def outputs(u, hf):
                pe.wait_ge(pt_ready, nth_half(u, hf))
                if hf == 0:
                    pe.wait_ge(v_ready, u)
                for j in range(HS // 2):
                    for g in range(G):
                        for par in range(2):
                            r = slice(par * KW, (par + 1) * KW)
                            at = (j * G + g) * VC
                            jj = hf * (HS // 2) + j
                            last = three(m[:, par, at:at + VC], pt_hi[r, g, j, :], pt_lo[r, g, j, :],
                                         v_hi[r, jj, g, :], v_lo[r, jj, g, :], start=(j == 0 and g == 0))
                last.then_inc(pv_done, 1)

            def project(u):
                pe.wait_ge(ot_ready, nth_half(u, 1))
                for t in range(TT):
                    cols = slice(t * P, (t + 1) * P)
                    last = three(m[:, 2, cols], ot_hi[:, cols], ot_lo[:, cols],
                                 aw_hi[:, 2 * P:3 * P], aw_lo[:, 2 * P:3 * P], start=(t == 0))
                last.then_inc(out_ready, 1)

            def unit(u, halves=(), first=False, last=False):
                for s in range(NE):
                    for q in range(FC):
                        i = FC * s + q
                        first_product(u, s, q)
                        if s > 0:
                            second_product(u, s - 1, q)
                        elif not first:
                            second_product(u - 1, NE - 1, q)
                        if 0 in halves:
                            if i == PE_AT["turn_att"]:
                                pe.wait_ge(c_used, u + 1)
                                turn(att, u, 2)
                            if i == PE_AT["qk"]:
                                if 1 in halves:
                                    pe.wait_ge(o_done, nth_half(u, 1))
                                queries_keys(u)
                            if i == PE_AT["v"]:
                                values(u)
                        for hf in halves:
                            if i == PE_AT["scores"][hf]:
                                scores(u, hf)
                            if i == PE_AT["turn_p"][hf]:
                                turn_probs(u, hf)
                            if i == PE_AT["pv"][hf]:
                                outputs(u, hf)
                        if 1 in halves and i == PE_AT["project"]:
                            if 0 in halves:
                                pe.wait_ge(v32_done, u)
                            else:
                                pe.wait_ge(c_used, u + 1)
                            project(u)
                        if not last:
                            if i == PE_AT["turn_pre"]:
                                if 0 in halves:
                                    pe.wait_ge(v32_done, u)
                                if 1 in halves:
                                    pe.wait_ge(x_attended, u - 1)
                                if not halves:
                                    pe.wait_ge(c_used, u + 1)
                                turn(pre, u + 2, 2)
                            if i == PE_AT["logits"]:
                                logits(u + 1)
                        if i == PE_AT["turn_c"]:
                            turn_c(u)
                        if first:
                            if i == PE_AT["logits0"]:
                                logits(0)
                            if i == PE_AT["turn_w"]:
                                turn_weights()

            pe.wait_ge(made, 3)
            pe.wait_ge(gate_loaded, 16)
            pe.transpose(m[:, 1, 0:E], gate_raw[:, :], ident[0:E, 0:E]).then_inc(gate_turned, 1)
            turn(pre, 1, 2)
            unit(0, first=True)
            unit(1, halves=(0,))
            with pe.Fori(2, NBLK + 1) as u:
                unit(u, halves=(0, 1))
            unit(NBLK + 1, halves=(1,))
            unit(NBLK + 2)
            unit(NU - 1, last=True)
            for q in range(FC):
                second_product(NU - 1, NE - 1, q)

        @block.scalar
        def _(act):
            def gelu(u, e, c):
                n = 4 * e + c
                act.wait_ge(z_ready, u * CH + n + 1)
                wait(act, h_ready, u * CH + n + 1 - H32)
                bank, bias = z[:, n % ZB, :], b1[:, e, c:c + 1]
                op = act.activation(h32[:, n % H32, :], bank, ACT.Gelu, bias=bias, scale=1 / WS)
                if c < FC - 1:
                    op = act.activation(h_hi[:, e % HB, c, :], bank, ACT.Gelu, bias=bias, scale=1 / WS)
                op.then_inc(gelu_done, 1)

            def split_w1(e):
                act.wait_ge(w1_loaded[e], 16)
                act.activation(w1_hi[:, e], w1_raw[:, e].rearrange("h (p c) -> h c p", c=FC), ACT.Copy, scale=WS)\
                    .then_inc(w1_hi_done, 1)

            def split_w2(e):
                act.wait_ge(w2_loaded[e], 16)
                act.activation(w2_hi[:, e].rearrange("p c h -> p (c h)"), w2_raw[:, e], ACT.Copy, scale=WS)\
                    .then_inc(w2_hi_done, 1)

            def normed_hi(n, count, to, bank):
                act.wait_ge(n.s_t, count)
                act.activation(to, m[:, bank, :], ACT.Copy).then_inc(n.s_hi, 1)

            def tanh(v):
                act.wait_ge(gate_step, v * STEPS + STEPS - 1)
                act.activation(th[:, :, :], dd[:, :, :], ACT.Tanh).then_inc(th_ready, 1)

            def keep_c(v):
                act.wait_ge(c_turned, v + 1)
                act.activation(c3t[:, :], m[0:96, 2, 0:BT // 2].bitcast(F16), ACT.Copy).then_inc(c_used, 1)

            def unit(u, halves=(), first=False, last=False):
                for s in range(NE):
                    for q in range(FC):
                        i = FC * s + q
                        gelu(u, s, q)
                        if 0 in halves:
                            if i == ACT_AT["hi_att"]:
                                normed_hi(att, u, xa_hi[:, WIN:], 2)
                            if i == ACT_AT["q32"]:
                                act.wait_ge(qk_done, u)
                                act.activation(q32[:, :], m[:, 0, :], ACT.Identity, bias=bq4[:, :], scale=0.25 / WS)
                                act.activation(k32[:, :], m[:, 1, :], ACT.Identity, bias=bk[:, :], scale=1 / WS)\
                                    .then_inc(q32_ready, 1)
                        for hf in halves:
                            if i == ACT_AT["exp"][hf]:
                                act.wait_ge(p_ready, nth_half(u, hf))
                                act.activation(pe_[:, :], pe_[:, :], ACT.Exp).then_inc(exp_done, 1)
                            if i == ACT_AT["pt_hi"][hf]:
                                act.wait_ge(p_turned, nth_half(u, hf))
                                act.activation(pt_hi[:, :, :, :].rearrange("p g j k -> p g (j k)"), m[:, 0:2, :],
                                               ACT.Copy).then_inc(pt_hi_done, 1)
                        if not last:
                            if i == ACT_AT["hi_pre"]:
                                normed_hi(pre, u + 2, slot(xt_hi, u + 1), 2)
                            if i == ACT_AT["tanh"]:
                                tanh(u + 1)
                        if i == ACT_AT["c3t"]:
                            keep_c(u)
                        if first:
                            if i == ACT_AT["tanh0"]:
                                tanh(0)
                            if q == 1 and s < NE - 2:
                                split_w1(s + 2)
                            if q == 3 and s < NE - 1:
                                split_w2(s + 1)
                            if i == ACT_AT["w_hi"]:
                                act.wait_ge(aw_turned, 1)
                                act.activation(aw_hi[:, :], m[:, 0, 0:AW], ACT.Copy, scale=WS).then_inc(aw_hi_done, 1)
                                act.activation(bq4[:, :], bq[:, :], ACT.Copy, scale=0.25).then_inc(aw_hi_done, 1)

            split_w1(0)
            act.wait_ge(gate_turned, 1)
            act.activation(gate_hi[:, :], m[:, 1, 0:E], ACT.Copy, scale=WS).then_inc(gate_hi_done, 1)
            normed_hi(pre, 1, slot(xt_hi, 0), 2)
            split_w1(1)
            split_w2(0)
            act.wait_ge(b1_loaded, 32)
            unit(0, first=True)
            act.wait_ge(aw_hi_done, 2)
            unit(1, halves=(0,))
            with act.Fori(2, NBLK + 1) as u:
                unit(u, halves=(0, 1))
            unit(NBLK + 1, halves=(1,))
            unit(NBLK + 2)
            unit(NU - 1, last=True)

        @block.vector
        def _(dve):
            def statistics(n, count, tokens):
                for t in range(TT):
                    op = dve.bn_stats(n.stats[:, t, :], tokens[:, t, :])
                op.then_inc(n.s_stats, 1)

            def variances(n, count):
                for t in range(TT):
                    op = dve.bn_aggr(n.mv[:, t, :], n.stats[:, t, :])
                op.then_inc(n.s_aggr, 1)
                dve.wait_ge(n.s_aggr, count)
                dve.tensor_scalar(n.ve[:, :], n.mv[:, :, 1], EPS, None, ALU.add).then_inc(n.s_var, 1)

            def normalize(n, count, tokens):
                dve.wait_ge(n.s_rstd, count)
                for t in range(TT):
                    op = dve.tensor_scalar(n.xn[:, t, :], tokens[:, t, :], n.mv[:, t, 0:1], n.rstd[:, t:t + 1],
                                           ALU.subtract, ALU.mult)
                op.then_inc(n.s_xn, 1)

            def normed_lo(n, count, to, hi, bank):
                dve.wait_ge(n.s_hi, count)
                dve.tensor_tensor(to, m[:, bank, :], hi, ALU.subtract).then_inc(n.s_xt, 1)

            def hidden(u, e, c):
                n = 4 * e + c
                dve.wait_ge(gelu_done, u * CH + n + 1)
                hi, src = h_hi[:, e % HB, c, :], h32[:, n % H32, :]
                if c == FC - 1:
                    dve.tensor_copy(hi, src).then_inc(h_hi_done, 1)
                    dve.wait_ge(h_hi_done, u * NE + e + 1)
                dve.tensor_tensor(h_lo[:, e % HB, c, :], src, hi, ALU.subtract).then_inc(h_ready, 1)

            def combine(u, e, final=False):
                dve.wait_ge(y_ready, u * NE + e + 1)
                wait(dve, y_used, u * NE + e)
                if e == 0:
                    dve.wait_ge(s_cur_ready, u + 1)
                tokens = slot(x, u)
                if e == SHARED and not final:
                    op = dve.scalar_tensor_tensor(tokens, y_bank(e).rearrange("p (t d) -> p t d", d=D), 0.5 / WS,
                                                  tokens, ALU.mult, ALU.add)
                for t in range(TT if e != SHARED or final else 0):
                    scale = 0.5 / WS if e == SHARED else s_cur[:, t, e:e + 1]
                    op = dve.scalar_tensor_tensor(tokens[:, t, :], y_bank(e)[:, t * P:(t + 1) * P], scale,
                                                  tokens[:, t, :], ALU.mult, ALU.add)
                    if final:
                        op.then_inc(last_tile, 1)
                if not final:
                    op.then_inc(y_used, 1)

            def router(v, step):
                if step > 0:
                    dve.wait_ge(gate_step, v * STEPS + step)
                if step == 0:
                    dve.wait_ge(lg_ready, v + 1)
                    op = dve.tensor_scalar(lg[:, :, :], m[:, 2, 0:TT * E].rearrange("p (t e) -> p t e", e=E),
                                           1 / WS, None, ALU.mult)
                if step == 1:
                    op = dve.tensor_tensor(pair[:, :, :, :], lg[:, :, :].unsqueeze(2).broadcast_to([P, TT, E, E]),
                                           lg[:, :, :].unsqueeze(3).broadcast_to([P, TT, E, E]), ALU.subtract)
                if step == 2:
                    op = dve.tensor_tensor(cmp[:, :, :, :], pair[:, :, :, :],
                                           before[:, :, :].unsqueeze(1).broadcast_to([P, TT, E, E]), ALU.is_ge)
                if step == 3:
                    op = dve.tensor_reduce(rank[:, :, :], cmp[:, :, :, :], AX.X, ALU.add)
                if step == 4:
                    op = dve.tensor_scalar(sel[:, :, :], rank[:, :, :], 1.5, 0.25 / WS, ALU.is_lt, ALU.mult)
                if step == 5:
                    op = dve.tensor_tensor(sl[:, :, :], sel[:, :, :], lg[:, :, :], ALU.mult)
                if step == 6:
                    op = dve.tensor_reduce(top[:, :], sl[:, :, :], AX.X, ALU.add)
                if step == 7:
                    op = dve.scalar_tensor_tensor(dd[:, :, :], top[:, :].unsqueeze(2).broadcast_to([P, TT, E]),
                                                  -2.0 * WS, lg[:, :, :], ALU.mult, ALU.add)
                if step == 8:
                    dve.wait_ge(th_ready, v + 1)
                    op = dve.scalar_tensor_tensor(s_next[:, :, :], th[:, :, :], 1.0, sel[:, :, :], ALU.add, ALU.mult)
                op.then_inc(gate_step, 1)

            def weights_c(v):
                dve.wait_ge(gate_step, v * STEPS + STEPS)
                dve.tensor_scalar(c3[:, :, 0:E], s_next[:, :, :], 2.0 * WS, None, ALU.mult).then_inc(c_step, 1)
                dve.wait_ge(c_step, v + 1)
                dve.scalar_tensor_tensor(c3[:, :, 32:32 + E], s_next[:, :, :], 2.0 * WS, c3[:, :, 0:E],
                                         ALU.mult, ALU.subtract)
                dve.tensor_copy(c3[:, :, 64:64 + E], c3[:, :, 0:E]).then_inc(c_ready, 1)

            def split_w1(e):
                dve.wait_ge(w1_hi_done, e + 1)
                dve.scalar_tensor_tensor(w1_lo[:, e], w1_raw[:, e].rearrange("h (p c) -> h c p", c=FC), WS,
                                         w1_hi[:, e], ALU.mult, ALU.subtract).then_inc(w1_split, 1)

            def split_w2(e):
                dve.wait_ge(w2_hi_done, e + 1)
                dve.scalar_tensor_tensor(w2_lo[:, e].rearrange("p c h -> p (c h)"), w2_raw[:, e], WS,
                                         w2_hi[:, e].rearrange("p c h -> p (c h)"), ALU.mult, ALU.subtract)\
                    .then_inc(w2_split, 1)

            def split_b2():
                dve.wait_ge(b2_loaded, 6 * 16)
                dve.tensor_scalar(b2_hi[:, :], b2_raw[:, :], WS, None, ALU.mult).then_inc(b2_step, 1)
                dve.wait_ge(b2_step, 1)
                dve.tensor_copy(b2_st[0:64, :], b2_hi[0:64, :])
                dve.scalar_tensor_tensor(b2_st[64:96, :], b2_raw[64:96, :], WS, b2_hi[64:96, :],
                                         ALU.mult, ALU.subtract).then_inc(b2_ready, 1)

            def split_qk(u):
                dve.wait_ge(q32_ready, u)
                dve.tensor_copy(q_hi[:, :], q32[:, :])
                dve.tensor_copy(k_hi[:, WIN:], k32[:, :]).then_inc(q_hi_done, 1)
                dve.wait_ge(q_hi_done, u)
                dve.tensor_tensor(q_lo[:, :], q32[:, :], q_hi[:, :], ALU.subtract)
                dve.tensor_tensor(k_lo[:, WIN:], k32[:, :], k_hi[:, WIN:], ALU.subtract).then_inc(q_split, 1)

            def keep_values(u):
                dve.wait_ge(v_done, u)
                dve.scalar_tensor_tensor(v32[:, :, :], m[:, 2, 0:HS * KVD].rearrange("p (j c) -> p j c", c=KVD), 1 / WS,
                                         bv[:, :].unsqueeze(1).broadcast_to([P, HS, KVD]), ALU.mult, ALU.add)\
                    .then_inc(v32_done, 1)
                dve.wait_ge(v32_done, u)
                src = v32[:, :, :].rearrange("p j (g d) -> p j g d", d=HD)
                dve.tensor_copy(v_hi[:, :, :, 0:HD], src).then_inc(v_hi_done, 1)
                dve.wait_ge(v_hi_done, u)
                dve.tensor_tensor(v_lo[:, :, :, 0:HD], src, v_hi[:, :, :, 0:HD], ALU.subtract).then_inc(v_ready, 1)

            def softmax_max(u, hf):
                dve.wait_ge(s_ready, nth_half(u, hf))
                dve.tensor_reduce(mx[:, :], m[:, 0:2, :].rearrange("p g (s k) -> p (g s) k", k=KW), AX.X, ALU.max)\
                    .then_inc(mx_done, 1)
                dve.wait_ge(mx_done, nth_half(u, hf))
                dve.tensor_scalar(mxs[:, :], mx[:, :], sink[:, 0:1], None, ALU.max).then_inc(mxs_done, 1)

            def softmax_less_max(u, hf):
                dve.wait_ge(mxs_done, nth_half(u, hf))
                dve.tensor_tensor(pe_[:, 0:NS * KW].rearrange("p (s k) -> p s k", k=KW),
                                  m[:, 0:2, :].rearrange("p g (s k) -> p (g s) k", k=KW),
                                  mxs[:, :].unsqueeze(2).broadcast_to([P, NS, KW]), ALU.subtract)
                dve.tensor_scalar(pe_[:, NS * KW:], mxs[:, :], -1.0, sink[:, 0:1], ALU.mult, ALU.add)\
                    .then_inc(p_ready, 1)

            def probs_lo(u, hf):
                dve.wait_ge(pt_hi_done, nth_half(u, hf))
                dve.tensor_tensor(pt_lo[:, :, :, :].rearrange("p g j k -> p g (j k)"), m[:, 0:2, :],
                                  pt_hi[:, :, :, :].rearrange("p g j k -> p g (j k)"), ALU.subtract)\
                    .then_inc(pt_ready, 1)

            def outputs_norm(u, hf):
                n = nth_half(u, hf)
                pv = m[:, 0:2, 0:HS // 2 * G * VC].rearrange("p a (j g c) -> p a j g c", g=G, c=VC)
                dve.wait_ge(pv_done, n)
                dve.tensor_tensor(den[:, :, :, :], pv[:, :, :, :, HD],
                                  pe_[:, NS * KW:].rearrange("p (g j a) -> p a j g", a=2, g=G), ALU.add)\
                    .then_inc(den_done, 1)
                dve.wait_ge(den_done, n)
                dve.reciprocal(rden[:, :, :, :], den[:, :, :, :]).then_inc(rden_done, 1)
                dve.wait_ge(rden_done, n)
                for par in range(2):
                    op = dve.tensor_tensor(o32[:, par::2, :, :], pv[:, par, :, :, 0:HD],
                                           rden[:, par].unsqueeze(3).broadcast_to([P, HS // 2, G, HD]), ALU.mult)
                op.then_inc(o_done, 1)

            def outputs_turn(u, hf):
                n = nth_half(u, hf)
                cols = slice(hf * HS * WIN, (hf + 1) * HS * WIN)
                dve.wait_ge(o_done, n)
                dve.transpose(ot32[:, :], o32[:, :, :, :].rearrange("p s g d -> p (s g d)")).then_inc(ot_turned, 1)
                dve.wait_ge(ot_turned, n)
                dve.tensor_copy(ot_hi[:, cols], ot32[:, :]).then_inc(ot_hi_done, 1)
                dve.wait_ge(ot_hi_done, n)
                dve.tensor_tensor(ot_lo[:, cols], ot32[:, :], ot_hi[:, cols], ALU.subtract).then_inc(ot_ready, 1)

            def unit(u, halves=(), first=False, last=False):
                for s in range(NE):
                    for q in range(FC):
                        i = FC * s + q
                        if 0 in halves and i == DVE_AT["stats_att"]:
                            dve.wait_ge(y_used, u * NE)
                        if 0 in halves and i == DVE_AT["var_att"]:
                            dve.wait_ge(att.s_stats, u)
                        if not last and i == DVE_AT["var_pre"]:
                            dve.wait_ge(pre.s_stats, u + 2)
                        hidden(u, s, q)
                        if 0 in halves and i == DVE_AT["var_att"]:
                            variances(att, u)
                        if not last and i == DVE_AT["var_pre"]:
                            variances(pre, u + 2)
                        if q == 0:
                            if s >= 2:
                                combine(u, s - 2)
                            elif not first:
                                combine(u - 1, NE - 2 + s)
                        if 0 in halves:
                            if i == DVE_AT["stats_att"]:
                                statistics(att, u, slot(x, u - 1))
                            if i == DVE_AT["xn_att"]:
                                normalize(att, u, slot(x, u - 1))
                            if i == DVE_AT["lo_att"]:
                                normed_lo(att, u, xa_lo[:, WIN:], xa_hi[:, WIN:], 2)
                            if i == DVE_AT["split_qk"]:
                                split_qk(u)
                            if i == DVE_AT["v"]:
                                keep_values(u)
                        for hf in halves:
                            if i == DVE_AT["max"][hf]:
                                softmax_max(u, hf)
                            if i == DVE_AT["less"][hf]:
                                softmax_less_max(u, hf)
                            if i == DVE_AT["pt_lo"][hf]:
                                probs_lo(u, hf)
                            if i == DVE_AT["norm"][hf]:
                                outputs_norm(u, hf)
                            if i == DVE_AT["turn_o"][hf]:
                                outputs_turn(u, hf)
                        if 1 in halves and i == DVE_AT["xres"]:
                            dve.wait_ge(y_used, (u - 1) * NE)
                            dve.tensor_tensor(xres[:, :, :], slot(x, u - 2),
                                              bo[:, :].unsqueeze(1).broadcast_to([P, TT, D]), ALU.add)\
                                .then_inc(xres_done, 1)
                        if 1 in halves and i == DVE_AT["add"]:
                            dve.wait_ge(xres_done, u - 1)
                            dve.wait_ge(out_ready, u - 1)
                            dve.scalar_tensor_tensor(slot(x, u + NBLK - 2), m[:, 2, :].rearrange("p (t d) -> p t d", d=D),
                                                     1 / WS, xres[:, :, :], ALU.mult, ALU.add).then_inc(x_attended, 1)
                        if not last:
                            if i == DVE_AT["stats_pre"]:
                                if first:
                                    dve.wait_ge(x_loaded[1], 16)
                                elif isinstance(u, int) and u == 1:
                                    for b in range(2, NBLK):
                                        dve.wait_ge(x_loaded[b], 16)
                                statistics(pre, u + 2, slot(x, u + 1))
                            if i == DVE_AT["xn_pre"]:
                                normalize(pre, u + 2, slot(x, u + 1))
                            if i == DVE_AT["lo_pre"]:
                                normed_lo(pre, u + 2, slot(xt_lo, u + 1), slot(xt_hi, u + 1), 2)
                            for step in range(STEPS):
                                if i == DVE_AT["router"] + step + (step == STEPS - 1):
                                    router(u + 1, step)
                        if first:
                            for step in range(STEPS):
                                if i == DVE_AT["router0"] + (step > 3) + (step == STEPS - 1):
                                    router(0, step)
                        if i == DVE_AT["s_cur"]:
                            wait(dve, y_used, u * NE)
                            dve.wait_ge(gate_step, (u + 1) * STEPS)
                            dve.tensor_copy(s_cur[:, :, :], s_next[:, :, :]).then_inc(s_cur_ready, 1)
                        if i == DVE_AT["c"]:
                            weights_c(u)
                        if first:
                            if q == 1 and s < NE - 2:
                                split_w1(s + 2)
                            if q == 3 and s < NE - 1:
                                split_w2(s + 1)
                            if i == DVE_AT["b2"]:
                                split_b2()
                            if i == DVE_AT["wo"]:
                                dve.wait_ge(aw_loaded, 16 * (2 * G * HG + 7))
                                dve.tensor_copy(wo_perm[:, :].rearrange("p (h g d) -> p h g d", h=HG, g=G),
                                                wo_raw[:, :].rearrange("p (g h d) -> p h g d", h=HG, g=G))\
                                    .then_inc(wo_ready, 1)
                            if i == DVE_AT["w_lo"]:
                                dve.wait_ge(aw_hi_done, 1)
                                dve.scalar_tensor_tensor(aw_lo[:, :], m[:, 0, 0:AW], WS, aw_hi[:, :], ALU.mult,
                                                         ALU.subtract).then_inc(aw_ready, 1)

            dve.memset(b2_raw[:, :], 0.0).then_inc(b2_zero, 1)
            dve.memset(c3[:, :, :], 0.0).then_inc(dve_made, 1)
            dve.wait_ge(dve_made, 1)
            dve.memset(c3[:, :, E:E + 1], 1.0)
            dve.memset(c3[:, :, 64 + E:65 + E], 1.0)
            dve.memset(xa_hi[:, 0:WIN], 0.0)
            dve.memset(xa_lo[:, 0:WIN], 0.0)
            dve.memset(k_hi[:, 0:WIN], 0.0)
            dve.memset(k_lo[:, 0:WIN], 0.0)
            dve.memset(v_lo[:, :, :, HD:VC], 0.0)
            dve.memset(v_hi[:, :, :, HD:HD + 1], 1.0)
            dve.memset(v_hi[:, :, :, HD + 1:VC], 0.0)
            dve.wait_ge(x_loaded[0], 16)
            statistics(pre, 1, slot(x, 0))
            dve.wait_ge(pre.s_stats, 1)
            variances(pre, 1)
            dve.wait_ge(made, 3)
            dve.tensor_copy(ident16[:, :], ident[:, :])
            dve.tensor_copy(identb[:, :], ident[:, :])
            normalize(pre, 1, slot(x, 0))
            split_w1(0)
            dve.wait_ge(gate_hi_done, 1)
            dve.scalar_tensor_tensor(gate_lo[:, :], m[:, 1, 0:E], WS, gate_hi[:, :], ALU.mult, ALU.subtract)\
                .then_inc(gate_ready, 1)
            normed_lo(pre, 1, slot(xt_lo, 0), slot(xt_hi, 0), 2)
            split_w1(1)
            split_w2(0)
            dve.wait_ge(made, 6)
            unit(0, first=True)
            dve.wait_ge(made, 21)
            unit(1, halves=(0,))
            with dve.Fori(2, NBLK + 1) as u:
                unit(u, halves=(0, 1))
            unit(NBLK + 1, halves=(1,))
            unit(NBLK + 2)
            unit(NU - 1, last=True)
            combine(NU - 1, NE - 2)
            combine(NU - 1, NE - 1, final=True)


_INS = ["L0_attn_x", "L0_attn_sink_bias", "L0_attn_Wq", "L0_attn_bq", "L0_attn_Wk", "L0_attn_bk", "L0_attn_Wv",
        "L0_attn_bv", "L0_attn_Wo", "L0_attn_bo", "L0_ffn_gate_w", "L0_ffn_W1", "L0_ffn_b1", "L0_ffn_W2",
        "L0_ffn_b2", "L0_ffn_sW1", "L0_ffn_sb1", "L0_ffn_sW2", "L0_ffn_sb2"]
_OUTS = [((4, 512, 128), "float32")]


def kernel(**inputs):
    import numpy as _np
    import concourse.bacc as _bacc
    from concourse import mybir as _mybir
    from concourse.bass_utils import run_bass_kernel_spmd as _run

    nc = _bacc.Bacc("TRN2", target_bir_lowering=False, num_devices=1)
    arrays, args = {}, []
    for name in _INS:
        a = _np.ascontiguousarray(inputs[name])
        arrays[f"in_{name}_dram"] = a
        args.append(nc.dram_tensor(f"in_{name}_dram", a.shape, _mybir.dt.from_np(a.dtype), kind="ExternalInput").ap())
    for i, (shape, dtype) in enumerate(_OUTS):
        dt = _mybir.dt.from_np(_np.dtype(dtype))
        args.append(nc.dram_tensor(f"out_{i}_dram", shape, dt, kind="ExternalOutput").ap())
    macaron_kernel(nc, *args)
    r = _run(nc, [arrays], core_ids=[0])
    return r.results[0]["out_0_dram"]
```

```python
from collections import namedtuple
from contextlib import ExitStack

import concourse.bass as bass
from concourse import mybir

ALU = mybir.AluOpType
ACT = mybir.ActivationFunctionType
AX = mybir.AxisListType
F32 = mybir.dt.float32
F16 = mybir.dt.float16
BF16 = mybir.dt.bfloat16

P = 128
WS = 64.0
EPS = 1e-5
MASKED = -1e30

PE_AT = dict(turn_att=12, qk=15, v=15, scores=(23, 6), turn_p=(31, 10), pv=(34, 13), project=21, turn_pre=23,
             logits=27, turn_c=10)
ACT_AT = dict(hi_att=12, q32=15, exp=(27, 8), pt_hi=(30, 10), hi_pre=23, tanh=35, c3t=9)
DVE_AT = dict(stats_att=5, var_att=8, xn_att=8, lo_att=11, split_qk=15, v=18, max=(22, 5), less=(22, 7),
              pt_lo=(30, 10), norm=(32, 11), turn_o=(35, 13), xres=8, add=19, stats_pre=8, var_pre=11, xn_pre=19,
              lo_pre=23, router=25, s_cur=7, c=4)

PE_AT0 = dict(turn_pre=22, logits=26, turn_c=11, logits0=1, turn_w=31)
ACT_AT0 = dict(hi_pre=22, tanh=34, c3t=10, tanh0=5, w_hi=30, w1=0, w2=3)
DVE_AT0 = dict(stats_pre=8, var_pre=10, xn_pre=19, lo_pre=21, router=25, s_cur=5, c=7, router0=2, b2=16, wo=25,
               w_lo=32, w1=0, w2=3)


def macaron_kernel(nc, x_in, sink_in, wq_in, bq_in, wk_in, bk_in, wv_in, bv_in, wo_in, bo_in,
                   gate_in, w1_in, b1_in, w2_in, b2_in, sw1_in, sb1_in, sw2_in, sb2_in, out):
    NBLK, BT, D = x_in.shape
    E, _, F = w1_in.shape
    NE = E + 1
    SHARED = E
    TT = BT // P
    FC = F // P
    CH = NE * FC
    NU = 2 * NBLK
    KVD = wk_in.shape[0]
    HD = 16
    G = KVD // HD
    HG = D // HD // G
    WIN = 32
    STRIPS = BT // WIN
    HS = STRIPS // 2
    KW = 2 * WIN
    VC = HD + 2
    ZB, HB = 3, 3
    H32 = 4
    assert D == P and CH % ZB == 0 and NE % HB == 0 and CH % H32 == 0

    with ExitStack() as ctx:
        def sb(name, shape, dt=F32):
            return ctx.enter_context(nc.sbuf_tensor(name, shape, dt))

        def sem(name):
            return ctx.enter_context(nc.semaphore(name))

        z = ctx.enter_context(nc.psum_tensor("z", [P, ZB, BT], F32))
        y = ctx.enter_context(nc.psum_tensor("y", [P, 2, BT], F32))
        m = ctx.enter_context(nc.psum_tensor("m", [P, 3, BT], F32))

        x = sb("x", [P, NU, TT, D])
        w1_raw, w2_raw = sb("w1_raw", [P, NE, F]), sb("w2_raw", [P, NE, F])
        w1_hi, w1_lo = sb("w1_hi", [P, NE, FC, P], F16), sb("w1_lo", [P, NE, FC, P], F16)
        w2_hi, w2_lo = sb("w2_hi", [P, NE, FC, D], F16), sb("w2_lo", [P, NE, FC, D], F16)
        b1 = sb("b1", [P, NE, FC])
        xt_hi, xt_lo = sb("xt_hi", [P, NU, BT], F16), sb("xt_lo", [P, NU, BT], F16)
        h32 = sb("h32", [P, H32, BT])
        h_hi, h_lo = sb("h_hi", [P, HB, FC, BT], F16), sb("h_lo", [P, HB, FC, BT], F16)
        ident, ident16, identb = sb("ident", [P, P]), sb("ident16", [P, P], F16), sb("identb", [P, P], BF16)
        gate_raw = sb("gate_raw", [E, D])
        gate_hi, gate_lo = sb("gate_hi", [P, E], F16), sb("gate_lo", [P, E], F16)
        lg, dd, th, sel = (sb(n, [P, TT, E]) for n in ("lg", "dd", "th", "sel"))
        pair, cmp, before = sb("pair", [P, TT, E, E]), sb("cmp", [P, TT, E, E]), sb("before", [P, E, E])
        rank, sl, top = sb("rank", [P, TT, E]), sb("sl", [P, TT, E]), sb("top", [P, TT])
        s_next, s_cur = sb("s_next", [P, TT, E]), sb("s_cur", [P, TT, E])
        c3 = sb("c3", [P, TT, 96], F16)
        c3t = sb("c3t", [96, BT], F16)
        b2_raw, b2_hi = sb("b2_raw", [96, D]), sb("b2_hi", [96, D], F16)
        b2_st = sb("b2_st", [96, D], F16)
        wq_raw, wk_raw, wo_raw = sb("wq_raw", [P, D]), sb("wk_raw", [P, D]), sb("wo_raw", [P, D])
        wo_perm, wv_raw = sb("wo_perm", [P, D]), sb("wv_raw", [KVD, D])
        AW = 3 * P + KVD
        aw_hi, aw_lo = sb("aw_hi", [P, AW], F16), sb("aw_lo", [P, AW], F16)
        bq, bq4, bk = sb("bq", [P, 1]), sb("bq4", [P, 1]), sb("bk", [P, 1])
        bv, bo, sink = sb("bv", [P, KVD]), sb("bo", [P, D]), sb("sink", [P, 1])
        head = sb("head", [P, HG])
        win = sb("win", [P, HS + 1, KW], BF16)
        xa_hi, xa_lo = sb("xa_hi", [P, WIN + BT], F16), sb("xa_lo", [P, WIN + BT], F16)
        xres = sb("xres", [P, TT, D])
        q32, k32 = sb("q32", [P, BT]), sb("k32", [P, BT])
        q_hi, q_lo = sb("q_hi", [P, BT], F16), sb("q_lo", [P, BT], F16)
        k_hi, k_lo = sb("k_hi", [P, WIN + BT], F16), sb("k_lo", [P, WIN + BT], F16)
        qm_hi = sb("qm_hi", [P, STRIPS, HG, WIN], F16)
        qm_lo = sb("qm_lo", [P, STRIPS, HG, WIN], F16)
        v32 = sb("v32", [P, HS, KVD])
        v_hi, v_lo = sb("v_hi", [P, HS, G, 2, VC], F16), sb("v_lo", [P, HS, G, 2, VC], F16)
        NS = G * HS
        mx, mxs = sb("mx", [P, NS]), sb("mxs", [P, NS])
        pe_ = sb("p_exp", [P, NS * KW + NS])
        pt_hi, pt_lo = sb("pt_hi", [P, G, HS // 2, P], F16), sb("pt_lo", [P, G, HS // 2, P], F16)
        den, rden = sb("den", [P, HS // 2, G, 2]), sb("rden", [P, HS // 2, G, 2])
        o32 = sb("o32", [P, HS, G, HD])
        ot32 = sb("ot32", [P, HS * KVD])
        ot_hi, ot_lo = sb("ot_hi", [P, BT], F16), sb("ot_lo", [P, BT], F16)
        zero, warm = sb("zero", [P, 1]), sb("warm", [P, 1])
        half = sb("half", [P, TT])

        Norm = namedtuple("Norm", "stats mv ve rstd xn s_stats s_aggr s_var s_rstd s_xn s_t s_hi s_xt")

        def norm(n):
            return Norm(sb(n + "_stats", [P, TT, 6]), sb(n + "_mv", [P, TT, 2]), sb(n + "_ve", [P, TT]),
                        sb(n + "_rstd", [P, TT]), sb(n + "_xn", [P, TT, D]),
                        sem(n + "_stats_done"), sem(n + "_aggr_done"), sem(n + "_var_ready"),
                        sem(n + "_rstd_ready"), sem(n + "_xn_ready"), sem(n + "_turned"),
                        sem(n + "_hi_ready"), sem(n + "_xt_ready"))

        pre = norm("pre")
        att = norm("att")

        x_loaded = [sem(f"x_loaded{b}") for b in range(NBLK)]
        w1_loaded = [sem(f"w1_loaded{e}") for e in range(NE)]
        w2_loaded = [sem(f"w2_loaded{e}") for e in range(NE)]
        gate_loaded, b1_loaded, b2_loaded = sem("gate_loaded"), sem("b1_loaded"), sem("b2_loaded")
        aw_loaded = sem("aw_loaded")
        made = sem("made")
        dve_made = sem("dve_made")
        gate_turned, gate_hi_done, gate_ready = sem("gate_turned"), sem("gate_hi_done"), sem("gate_ready")
        w1_hi_done, w1_split = sem("w1_hi_done"), sem("w1_split")
        w2_hi_done, w2_split = sem("w2_hi_done"), sem("w2_split")
        b2_step, b2_zero, b2_ready = sem("b2_step"), sem("b2_zero"), sem("b2_ready")
        wo_ready, aw_turned, aw_hi_done, aw_ready = sem("wo_ready"), sem("aw_turned"), sem("aw_hi_done"), sem("aw_ready")
        z_ready = sem("z_ready")
        gelu_done = sem("gelu_done")
        act_hi_done = sem("act_hi_done")
        h_hi_done = sem("h_hi_done")
        h_ready = sem("h_ready")
        y_ready = sem("y_ready")
        y_used = sem("y_used")
        lg_ready, gate_step, th_ready = sem("lg_ready"), sem("gate_step"), sem("th_ready")
        c_step = sem("c_step")
        c_ready, c_turned, c_used = sem("c_ready"), sem("c_turned"), sem("c3t_ready")
        s_cur_ready = sem("s_cur_ready")
        qk_done, q32_ready, q_hi_done, q_ready = sem("qk_done"), sem("q32_ready"), sem("q_hi_done"), sem("q_ready")
        q_split = sem("q_split")
        v_done, v32_done, v_hi_done, v_ready = sem("v_done"), sem("v32_done"), sem("v_hi_done"), sem("v_ready")
        s_ready, mx_done, mxs_done, p_ready = sem("s_ready"), sem("mx_done"), sem("mxs_done"), sem("p_ready")
        exp_done, p_turned, pt_hi_done, pt_ready = sem("exp_done"), sem("p_turned"), sem("pt_hi_done"), sem("pt_ready")
        pv_done, den_done, rden_done, o_done = sem("pv_done"), sem("den_done"), sem("rden_done"), sem("o_done")
        ot_turned, ot_hi_done, ot_ready = sem("ot_turned"), sem("ot_hi_done"), sem("ot_ready")
        out_ready, xres_done, x_attended = sem("out_ready"), sem("xres_done"), sem("x_attended")
        last_tile, stored = sem("last_tile"), sem("stored")

        def slot(buf, u):
            if isinstance(u, int):
                return buf[:, u]
            view = buf[:, bass.ds(u, 1)]
            return view.rearrange("p a t d -> p (a t) d") if len(view.shape) == 4 else view.rearrange("p a t -> p (a t)")

        def wait(eng, s, value):
            if not isinstance(value, int) or value > 0:
                eng.wait_ge(s, value)

        def nth_half(u, hf):
            return 2 * u - 1 if hf == 0 else 2 * u - 2

        def nth_group(u, hf, g):
            return 2 * nth_half(u, hf) - 1 + g

        def hi_on_dve(e, c):
            return c == FC - 1 and e % 2 == 0

        def y_bank(e):
            return y[:, e % 2] if e != SHARED else m[:, 2]

        def strided(ap, offset, dims):
            return bass.AP(ap.tensor, offset, dims)

        DVE_HI = (NE + 1) // 2
        STEPS = 9
        AW_LOADS = 2 * G + 7

        block = ctx.enter_context(nc.Block())

        @block.sync
        def _(sp):
            def load_x(b):
                sp.dma_start(x[:, b], x_in[b].rearrange("(t p) d -> p t d", p=P)).then_inc(x_loaded[b], 16)

            def load_w1(e):
                src = sw1_in if e == SHARED else w1_in[e]
                sp.dma_start(w1_raw[:, e], src).then_inc(w1_loaded[e], 16)

            def load_w2(e):
                src = sw2_in if e == SHARED else w2_in[e]
                sp.dma_start(w2_raw[:, e], src.rearrange("(p c) h -> p (c h)", c=FC)).then_inc(w2_loaded[e], 16)

            load_x(0)
            load_w1(0)
            load_w2(0)
            for e in range(1, NE):
                load_w1(e)
                load_w2(e)
                if e == 4:
                    load_x(1)
            for b in range(2, NBLK):
                load_x(b)
            with sp.Fori(0, NBLK - 1) as b:
                sp.wait_ge(y_used, b * NE + NE * (NBLK + 1))
                sp.dma_start(out[bass.ds(b, 1)].rearrange("a (t p) d -> p (a t) d", p=P),
                             slot(x, b + NBLK)).then_inc(stored, 16)
            for t in range(TT):
                sp.wait_ge(last_tile, t + 1)
                sp.dma_start(out[NBLK - 1, t * P:(t + 1) * P], x[:, NU - 1, t]).then_inc(stored, 16)
            sp.wait_ge(stored, 16 * (NBLK - 1 + TT))

        @block.gpsimd
        def _(pool):
            pool.dma_start(gate_raw[:, :], gate_in).then_inc(gate_loaded, 16)
            pool.memset(half[:, :], -0.5).then_inc(made, 1)
            pool.memset(ident[:, :], 0.0).then_inc(made, 1)
            pool.wait_ge(made, 2)
            pool.affine_select(out=ident[:, :], in_=ident[:, :], compare_op=ALU.not_equal, fill=1.0,
                               base=0, pattern=[[-1, P]], channel_multiplier=1).then_inc(made, 1)

            def inv_std(n, count):
                pool.wait_ge(n.s_var, count)
                pool.tensor_tensor(n.rstd[:, :], n.ve[:, :], half[:, :], ALU.pow).then_inc(n.s_rstd, 1)

            def mask_heads(u, hf):
                pool.wait_ge(q_split, u)
                strips = slice(hf * HS, (hf + 1) * HS)
                for src, to in ((q_hi, qm_hi), (q_lo, qm_lo)):
                    queries = src[:, :].rearrange("p (s q) -> p s q", q=WIN)[:, strips]
                    pool.tensor_tensor(to[:, strips, 0, :], queries, head[:, 0:1].unsqueeze(2).broadcast_to([P, HS, WIN]),
                                       ALU.mult)
                    for h in range(1, HG):
                        op = pool.tensor_scalar(to[:, strips, h, :], queries, head[:, h:h + 1], None, ALU.mult)
                op.then_inc(q_ready, 1)

            inv_std(pre, 1)
            pool.memset(before[:, :, :], 0.0).then_inc(made, 1)
            pool.wait_ge(made, 4)
            pool.affine_select(out=before[:, :, :], in_=before[:, :, :], compare_op=ALU.is_gt, fill=1.2e-38,
                               base=0, pattern=[[1, E], [-1, E]], channel_multiplier=0).then_inc(made, 1)
            pool.wait_ge(made, 5)
            pool.affine_select(out=before[:, :, :], in_=before[:, :, :], compare_op=ALU.not_equal, fill=3e38,
                               base=0, pattern=[[1, E], [-1, E]], channel_multiplier=0).then_inc(made, 1)
            pool.wait_ge(b2_zero, 1)
            for p in range(0, 96, 32):
                pool.dma_start(b2_raw[p:p + E, :], b2_in).then_inc(b2_loaded, 16)
                pool.dma_start(b2_raw[p + E:p + E + 1, :], sb2_in.rearrange("(a d) -> a d", a=1)).then_inc(b2_loaded, 16)
            pool.dma_start(wq_raw[:, :], wq_in).then_inc(aw_loaded, 16)
            for g in range(G):
                r = g * HG * HD
                pool.dma_start(wk_raw[r:r + HG * HD, :], strided(wk_in, g * HD * D, [[0, HG], [D, HD], [1, D]]))\
                    .then_inc(aw_loaded, 16)
                pool.dma_start(bk[r:r + HG * HD, :], strided(bk_in, g * HD, [[0, HG], [1, HD], [1, 1]]))\
                    .then_inc(aw_loaded, 16)
            pool.dma_start(wv_raw[:, :], wv_in).then_inc(aw_loaded, 16)
            pool.dma_start(wo_raw[:, :], wo_in).then_inc(aw_loaded, 16)
            pool.dma_start(bq[:, :], bq_in.rearrange("(p a) -> p a", a=1)).then_inc(aw_loaded, 16)
            pool.dma_start(bv[:, :], strided(bv_in, 0, [[0, P], [1, KVD]])).then_inc(aw_loaded, 16)
            pool.dma_start(bo[:, :], strided(bo_in, 0, [[0, P], [1, D]])).then_inc(aw_loaded, 16)
            pool.dma_start(sink[:, :], strided(sink_in, 0, [[0, P], [1, 1]])).then_inc(aw_loaded, 16)
            inv_std(pre, 2)
            pool.memset(head[:, :], 1.0).then_inc(made, 1)
            pool.memset(win[:, :, :], 0.0).then_inc(made, 1)
            for g in range(G):
                rows = head[g * HG * HD:(g + 1) * HG * HD, :]
                pool.wait_ge(made, 8 + 2 * g)
                pool.affine_select(out=rows, in_=rows, compare_op=ALU.is_ge, fill=0.0, base=0,
                                   pattern=[[-HD, HG]], channel_multiplier=1).then_inc(made, 1)
                pool.wait_ge(made, 9 + 2 * g)
                pool.affine_select(out=rows, in_=rows, compare_op=ALU.is_ge, fill=0.0, base=HD - 1,
                                   pattern=[[HD, HG]], channel_multiplier=-1).then_inc(made, 1)
            for h in range(HG):
                rows = win[h * WIN:(h + 1) * WIN]
                pool.wait_ge(made, 12 + 2 * h)
                pool.affine_select(out=rows, in_=rows, compare_op=ALU.is_gt, fill=MASKED, base=0,
                                   pattern=[[0, HS + 1], [1, KW]], channel_multiplier=-1).then_inc(made, 1)
                pool.wait_ge(made, 13 + 2 * h)
                pool.affine_select(out=rows, in_=rows, compare_op=ALU.is_ge, fill=MASKED, base=WIN,
                                   pattern=[[0, HS + 1], [-1, KW]], channel_multiplier=1).then_inc(made, 1)
            pool.wait_ge(made, 20)
            pool.affine_select(out=win[:, 0, :], in_=win[:, 0, :], compare_op=ALU.is_ge, fill=MASKED,
                               base=-WIN, pattern=[[1, KW]], channel_multiplier=0).then_inc(made, 1)
            pool.wait_ge(made, 21)
            with pool.Fori(1, NBLK + 1) as u:
                inv_std(att, u)
                inv_std(pre, u + 2)
                mask_heads(u, 0)
                mask_heads(u, 1)
            with pool.Fori(NBLK + 1, NU - 1) as u:
                inv_std(pre, u + 2)

        @block.tensor
        def _(pe):
            def first_product(u, e, c):
                n = 4 * e + c
                if c == 0 and e == 0:
                    pe.wait_ge(pre.s_xt, u + 1)
                if c == 0 and isinstance(u, int) and u == 0:
                    pe.wait_ge(w1_split, e + 1)
                wait(pe, gelu_done, u * CH + n + 1 - ZB)
                bank = z[:, n % ZB, :]
                pe.matmul(bank, w1_hi[:, e, c, :], slot(xt_hi, u), start=True, stop=False)
                pe.matmul(bank, w1_hi[:, e, c, :], slot(xt_lo, u), start=False, stop=False)
                pe.matmul(bank, w1_lo[:, e, c, :], slot(xt_hi, u), start=False, stop=True).then_inc(z_ready, 1)

            def second_product(u, e, c):
                if c == 0:
                    if isinstance(u, int) and u == 0:
                        pe.wait_ge(w2_split, e + 1)
                    wait(pe, y_used, u * NE + e - (2 if e < 2 else 1))
                    if e == SHARED and not (isinstance(u, int) and u == NU - 1):
                        pe.wait_ge(gate_step, (u + 1) * STEPS + 1)
                pe.wait_ge(h_ready, u * CH + 4 * e + c + 1)
                for t in range(TT):
                    cols = slice(t * P, (t + 1) * P)
                    hi, lo, to = h_hi[:, e % HB, c, cols], h_lo[:, e % HB, c, cols], y_bank(e)[:, cols]
                    pe.matmul(to, hi, w2_hi[:, e, c, :], start=(c == 0 and t == 0), stop=False, skip_group_check=True)
                    pe.matmul(to, hi, w2_lo[:, e, c, :], start=False, stop=False, skip_group_check=True)
                    last = pe.matmul(to, lo, w2_hi[:, e, c, :], start=False, stop=(c == FC - 1), skip_group_check=True)
                if e == SHARED and c == FC - 1:
                    if isinstance(u, int) and u == 0:
                        pe.wait_ge(b2_ready, 1)
                    pe.wait_ge(c_used, u + 1)
                    for t in range(TT):
                        cols = slice(t * P, (t + 1) * P)
                        last = pe.matmul(y_bank(e)[:, cols], c3t[:, cols], b2_st[:, :], start=False, stop=True,
                                         skip_group_check=True)
                if c == FC - 1:
                    last.then_inc(y_ready, 1)

            def turn(n, count, bank):
                pe.wait_ge(n.s_xn, count)
                for t in range(TT):
                    last = pe.transpose(m[:, bank, t * P:(t + 1) * P], n.xn[:, t, :], ident[:, :])
                last.then_inc(n.s_t, 1)

            def three(to, a_hi, a_lo, b_hi, b_lo, start=True, stop=True):
                pe.matmul(to, a_hi, b_hi, start=start, stop=False, skip_group_check=True)
                pe.matmul(to, a_hi, b_lo, start=False, stop=False, skip_group_check=True)
                return pe.matmul(to, a_lo, b_hi, start=False, stop=stop, skip_group_check=True)

            def logits(v):
                pe.wait_ge(pre.s_xt, v + 1)
                if isinstance(v, int) and v == 0:
                    pe.wait_ge(gate_ready, 1)
                for t in range(TT):
                    cols = slice(t * P, (t + 1) * P)
                    last = three(m[:, 2, t * E:(t + 1) * E], slot(xt_hi, v)[:, cols], slot(xt_lo, v)[:, cols],
                                 gate_hi[:, :], gate_lo[:, :], start=(t == 0))
                last.then_inc(lg_ready, 1)

            def turn_c(v):
                wait(pe, y_used, v * NE)
                pe.wait_ge(c_ready, v + 1)
                for t in range(TT):
                    last = pe.transpose(m[0:96, 2, t * 64:(t + 1) * 64].bitcast(F16), c3[:, t, :], ident16[:, :])
                last.then_inc(c_turned, 1)

            def turn_weights():
                pe.wait_ge(aw_loaded, 16 * AW_LOADS)
                pe.transpose(m[:, 0, 0:P], wq_raw[:, :], ident[:, :])
                pe.transpose(m[:, 0, P:2 * P], wk_raw[:, :], ident[:, :])
                pe.wait_ge(wo_ready, 1)
                pe.transpose(m[:, 0, 2 * P:3 * P], wo_perm[:, :], ident[:, :])
                pe.transpose(m[:, 0, 3 * P:AW], wv_raw[:, :], ident[0:KVD, 0:KVD]).then_inc(aw_turned, 1)

            def queries_keys(u, other_half):
                pe.wait_ge(att.s_xt, u)
                if isinstance(u, int):
                    pe.wait_ge(aw_ready, 1)
                xh, xl = xa_hi[:, WIN:], xa_lo[:, WIN:]
                three(m[:, 1, :], aw_hi[:, P:2 * P], aw_lo[:, P:2 * P], xh, xl)
                if other_half:
                    pe.wait_ge(o_done, nth_half(u, 1))
                three(m[:, 0, :], aw_hi[:, 0:P], aw_lo[:, 0:P], xh, xl).then_inc(qk_done, 1)

            def values(u):
                pe.wait_ge(att.s_xt, u)
                if isinstance(u, int):
                    pe.wait_ge(aw_ready, 1)
                for j in range(HS):
                    for par in range(2):
                        at = slice(j * KW + par * WIN, j * KW + par * WIN + KW)
                        last = three(m[par * KW:(par + 1) * KW, 2, j * KVD:(j + 1) * KVD], xa_hi[:, at], xa_lo[:, at],
                                     aw_hi[:, 3 * P:AW], aw_lo[:, 3 * P:AW], start=(j == 0))
                last.then_inc(v_done, 1)

            def scores(u, hf):
                pe.wait_ge(q_ready, nth_half(u, hf))
                if hf == 1:
                    pe.wait_ge(o_done, nth_half(u, 1) - 1)
                for g in range(G):
                    pe.matmul(m[:, g, :], identb[:, :], win[:, hf:hf + HS, :].rearrange("p s k -> p (s k)"),
                              start=True, stop=False, skip_group_check=True)
                for i in range(HS):
                    s = hf * HS + i
                    for g in range(G):
                        r = slice(g * HG * HD, (g + 1) * HG * HD)
                        last = three(m[:, g, i * KW:(i + 1) * KW],
                                     qm_hi[r, s, :, :].rearrange("p h q -> p (h q)"),
                                     qm_lo[r, s, :, :].rearrange("p h q -> p (h q)"),
                                     k_hi[r, s * WIN:s * WIN + KW], k_lo[r, s * WIN:s * WIN + KW], start=False)
                last.then_inc(s_ready, 1)

            def turn_probs(u, hf):
                pe.wait_ge(exp_done, nth_half(u, hf))
                for g in range(G):
                    for j in range(HS // 2):
                        at = g * HS * KW + j * 2 * KW
                        last = pe.transpose(m[:, g, j * P:(j + 1) * P], pe_[:, at:at + 2 * KW], ident[:, :])
                    last.then_inc(p_turned, 1)

            def outputs(u, hf):
                if hf == 0:
                    pe.wait_ge(v_ready, u)
                for g in range(G):
                    pe.wait_ge(pt_ready, nth_group(u, hf, g))
                    for j in range(HS // 2):
                        at = (j * G + g) * 2 * VC
                        jj = hf * (HS // 2) + j
                        last = three(m[:, 0, at:at + 2 * VC], pt_hi[:, g, j, :], pt_lo[:, g, j, :],
                                     v_hi[:, jj, g, :, :].rearrange("p a c -> p (a c)"),
                                     v_lo[:, jj, g, :, :].rearrange("p a c -> p (a c)"), start=(j == 0 and g == 0))
                last.then_inc(pv_done, 1)

            def project(u):
                pe.wait_ge(ot_ready, nth_half(u, 1))
                for t in range(TT):
                    cols = slice(t * P, (t + 1) * P)
                    last = three(m[:, 2, cols], ot_hi[:, cols], ot_lo[:, cols],
                                 aw_hi[:, 2 * P:3 * P], aw_lo[:, 2 * P:3 * P], start=(t == 0))
                last.then_inc(out_ready, 1)

            def unit(u, halves=(), first=False, last=False):
                at = PE_AT0 if first else PE_AT
                for s in range(NE):
                    for q in range(FC):
                        i = FC * s + q
                        first_product(u, s, q)
                        if s > 0:
                            second_product(u, s - 1, q)
                        elif not first:
                            second_product(u - 1, NE - 1, q)
                        if 0 in halves:
                            if i == at["turn_att"]:
                                pe.wait_ge(c_used, u + 1)
                                turn(att, u, 2)
                            if i == at["qk"]:
                                queries_keys(u, 1 in halves)
                            if i == at["v"]:
                                values(u)
                        for hf in halves:
                            if i == at["scores"][hf]:
                                scores(u, hf)
                            if i == at["turn_p"][hf]:
                                turn_probs(u, hf)
                            if i == at["pv"][hf]:
                                outputs(u, hf)
                        if 1 in halves and i == at["project"]:
                            if 0 in halves:
                                pe.wait_ge(v32_done, u)
                            else:
                                pe.wait_ge(c_used, u + 1)
                            project(u)
                        if not last:
                            if i == at["turn_pre"]:
                                if 0 in halves:
                                    pe.wait_ge(v32_done, u)
                                if 1 in halves:
                                    pe.wait_ge(x_attended, u - 1)
                                if not halves:
                                    pe.wait_ge(c_used, u + 1)
                                turn(pre, u + 2, 2)
                            if i == at["logits"]:
                                logits(u + 1)
                        if i == at["turn_c"]:
                            turn_c(u)
                        if first:
                            if i == at["logits0"]:
                                logits(0)
                            if i == at["turn_w"]:
                                turn_weights()

            pe.wait_ge(made, 3)
            pe.wait_ge(gate_loaded, 16)
            pe.transpose(m[:, 1, 0:E], gate_raw[:, :], ident[0:E, 0:E]).then_inc(gate_turned, 1)
            turn(pre, 1, 2)
            unit(0, first=True)
            unit(1, halves=(0,))
            with pe.Fori(2, NBLK + 1) as u:
                unit(u, halves=(0, 1))
            unit(NBLK + 1, halves=(1,))
            unit(NBLK + 2)
            unit(NU - 1, last=True)
            for q in range(FC):
                second_product(NU - 1, NE - 1, q)

        @block.scalar
        def _(act):
            def gelu(u, e, c):
                n = 4 * e + c
                act.wait_ge(z_ready, u * CH + n + 1)
                wait(act, h_ready, u * CH + n + 1 - H32)
                bank, bias = z[:, n % ZB, :], b1[:, e, c:c + 1]
                act.activation(h32[:, n % H32, :], bank, ACT.Gelu, bias=bias, scale=1 / WS).then_inc(gelu_done, 1)
                if not hi_on_dve(e, c):
                    act.wait_ge(gelu_done, u * CH + n + 1)
                    act.activation(h_hi[:, e % HB, c, :], h32[:, n % H32, :], ACT.Copy).then_inc(act_hi_done, 1)

            def split_w1(e):
                act.wait_ge(w1_loaded[e], 16)
                act.activation(w1_hi[:, e], w1_raw[:, e].rearrange("h (p c) -> h c p", c=FC), ACT.Copy, scale=WS)\
                    .then_inc(w1_hi_done, 1)

            def split_w2(e):
                act.wait_ge(w2_loaded[e], 16)
                act.activation(w2_hi[:, e].rearrange("p c h -> p (c h)"), w2_raw[:, e], ACT.Copy, scale=WS)\
                    .then_inc(w2_hi_done, 1)

            def normed_hi(n, count, to, bank):
                act.wait_ge(n.s_t, count)
                act.activation(to, m[:, bank, :], ACT.Copy).then_inc(n.s_hi, 1)

            def tanh(v):
                act.wait_ge(gate_step, v * STEPS + STEPS - 1)
                act.activation(th[:, :, :], dd[:, :, :], ACT.Tanh).then_inc(th_ready, 1)

            def keep_c(v):
                act.wait_ge(c_turned, v + 1)
                act.activation(c3t[:, :], m[0:96, 2, 0:BT // 2].bitcast(F16), ACT.Copy).then_inc(c_used, 1)

            def unit(u, halves=(), first=False, last=False):
                at = ACT_AT0 if first else ACT_AT
                for s in range(NE):
                    for q in range(FC):
                        i = FC * s + q
                        gelu(u, s, q)
                        if 0 in halves:
                            if i == at["hi_att"]:
                                normed_hi(att, u, xa_hi[:, WIN:], 2)
                            if i == at["q32"]:
                                act.wait_ge(qk_done, u)
                                act.activation(q32[:, :], m[:, 0, :], ACT.Identity, bias=bq4[:, :], scale=0.25 / WS)
                                act.activation(k32[:, :], m[:, 1, :], ACT.Identity, bias=bk[:, :], scale=1 / WS)\
                                    .then_inc(q32_ready, 1)
                        for hf in halves:
                            if i == at["exp"][hf]:
                                act.wait_ge(p_ready, nth_half(u, hf))
                                act.activation(pe_[:, :], pe_[:, :], ACT.Exp).then_inc(exp_done, 1)
                            if i == at["pt_hi"][hf]:
                                for g in range(G):
                                    act.wait_ge(p_turned, nth_group(u, hf, g))
                                    act.activation(pt_hi[:, g, :, :].rearrange("p j k -> p (j k)"), m[:, g, :],
                                                   ACT.Copy).then_inc(pt_hi_done, 1)
                        if not last:
                            if i == at["hi_pre"]:
                                normed_hi(pre, u + 2, slot(xt_hi, u + 1), 2)
                            if i == at["tanh"]:
                                tanh(u + 1)
                        if i == at["c3t"]:
                            keep_c(u)
                        if first:
                            if i == at["tanh0"]:
                                tanh(0)
                            if q == at["w1"] and s < NE - 2:
                                split_w1(s + 2)
                            if q == at["w2"] and s < NE - 1:
                                split_w2(s + 1)
                            if i == at["w_hi"]:
                                act.wait_ge(aw_turned, 1)
                                act.activation(aw_hi[:, :], m[:, 0, 0:AW], ACT.Copy, scale=WS).then_inc(aw_hi_done, 1)
                                act.activation(bq4[:, :], bq[:, :], ACT.Copy, scale=0.25).then_inc(aw_hi_done, 1)

            act.dma_start(b1[:, 0:E], b1_in.rearrange("e (p c) -> p e c", c=FC)).then_inc(b1_loaded, 16)
            act.dma_start(b1[:, SHARED], sb1_in.rearrange("(p c) -> p c", c=FC)).then_inc(b1_loaded, 16)
            act.wait_ge(b2_zero, 1)
            act.activation(warm[:, :], zero[:, :], ACT.Gelu)
            split_w1(0)
            act.wait_ge(gate_turned, 1)
            act.activation(gate_hi[:, :], m[:, 1, 0:E], ACT.Copy, scale=WS).then_inc(gate_hi_done, 1)
            normed_hi(pre, 1, slot(xt_hi, 0), 2)
            split_w1(1)
            split_w2(0)
            act.wait_ge(b1_loaded, 32)
            unit(0, first=True)
            act.wait_ge(aw_hi_done, 2)
            unit(1, halves=(0,))
            with act.Fori(2, NBLK + 1) as u:
                unit(u, halves=(0, 1))
            unit(NBLK + 1, halves=(1,))
            unit(NBLK + 2)
            unit(NU - 1, last=True)

        @block.vector
        def _(dve):
            def statistics(n, count, tokens):
                for t in range(TT):
                    op = dve.bn_stats(n.stats[:, t, :], tokens[:, t, :])
                op.then_inc(n.s_stats, 1)

            def variances(n, count):
                for t in range(TT):
                    op = dve.bn_aggr(n.mv[:, t, :], n.stats[:, t, :])
                op.then_inc(n.s_aggr, 1)
                dve.wait_ge(n.s_aggr, count)
                dve.tensor_scalar(n.ve[:, :], n.mv[:, :, 1], EPS, None, ALU.add).then_inc(n.s_var, 1)

            def normalize(n, count, tokens):
                dve.wait_ge(n.s_rstd, count)
                for t in range(TT):
                    op = dve.tensor_scalar(n.xn[:, t, :], tokens[:, t, :], n.mv[:, t, 0:1], n.rstd[:, t:t + 1],
                                           ALU.subtract, ALU.mult)
                op.then_inc(n.s_xn, 1)

            def normed_lo(n, count, to, hi, bank):
                dve.wait_ge(n.s_hi, count)
                dve.tensor_tensor(to, m[:, bank, :], hi, ALU.subtract).then_inc(n.s_xt, 1)

            def hidden(u, e, c):
                n = 4 * e + c
                if hi_on_dve(e, c):
                    dve.wait_ge(gelu_done, u * CH + n + 1)
                else:
                    dve.wait_ge(act_hi_done, u * (CH - DVE_HI) + n + 1 - (e + 1) // 2)
                hi, src = h_hi[:, e % HB, c, :], h32[:, n % H32, :]
                if hi_on_dve(e, c):
                    dve.tensor_copy(hi, src).then_inc(h_hi_done, 1)
                    dve.wait_ge(h_hi_done, u * DVE_HI + e // 2 + 1)
                dve.tensor_tensor(h_lo[:, e % HB, c, :], src, hi, ALU.subtract).then_inc(h_ready, 1)

            def combine(u, e, final=False):
                dve.wait_ge(y_ready, u * NE + e + 1)
                wait(dve, y_used, u * NE + e)
                if e == 0:
                    dve.wait_ge(s_cur_ready, u + 1)
                tokens = slot(x, u)
                if e == SHARED and not final:
                    op = dve.scalar_tensor_tensor(tokens, y_bank(e).rearrange("p (t d) -> p t d", d=D), 0.5 / WS,
                                                  tokens, ALU.mult, ALU.add)
                for t in range(TT if e != SHARED or final else 0):
                    scale = 0.5 / WS if e == SHARED else s_cur[:, t, e:e + 1]
                    op = dve.scalar_tensor_tensor(tokens[:, t, :], y_bank(e)[:, t * P:(t + 1) * P], scale,
                                                  tokens[:, t, :], ALU.mult, ALU.add)
                    if final:
                        op.then_inc(last_tile, 1)
                if not final:
                    op.then_inc(y_used, 1)

            def router(v, step):
                if step > 0:
                    dve.wait_ge(gate_step, v * STEPS + step)
                if step == 0:
                    dve.wait_ge(lg_ready, v + 1)
                    op = dve.tensor_scalar(lg[:, :, :], m[:, 2, 0:TT * E].rearrange("p (t e) -> p t e", e=E),
                                           1 / WS, None, ALU.mult)
                if step == 1:
                    op = dve.tensor_tensor(pair[:, :, :, :], lg[:, :, :].unsqueeze(2).broadcast_to([P, TT, E, E]),
                                           lg[:, :, :].unsqueeze(3).broadcast_to([P, TT, E, E]), ALU.subtract)
                if step == 2:
                    op = dve.tensor_tensor(cmp[:, :, :, :], pair[:, :, :, :],
                                           before[:, :, :].unsqueeze(1).broadcast_to([P, TT, E, E]), ALU.is_ge)
                if step == 3:
                    op = dve.tensor_reduce(rank[:, :, :], cmp[:, :, :, :], AX.X, ALU.add)
                if step == 4:
                    op = dve.tensor_scalar(sel[:, :, :], rank[:, :, :], 1.5, 0.25 / WS, ALU.is_lt, ALU.mult)
                if step == 5:
                    op = dve.tensor_tensor(sl[:, :, :], sel[:, :, :], lg[:, :, :], ALU.mult)
                if step == 6:
                    op = dve.tensor_reduce(top[:, :], sl[:, :, :], AX.X, ALU.add)
                if step == 7:
                    op = dve.scalar_tensor_tensor(dd[:, :, :], top[:, :].unsqueeze(2).broadcast_to([P, TT, E]),
                                                  -2.0 * WS, lg[:, :, :], ALU.mult, ALU.add)
                if step == 8:
                    dve.wait_ge(th_ready, v + 1)
                    op = dve.scalar_tensor_tensor(s_next[:, :, :], th[:, :, :], 1.0, sel[:, :, :], ALU.add, ALU.mult)
                op.then_inc(gate_step, 1)

            def weights_c(v):
                dve.wait_ge(gate_step, v * STEPS + STEPS)
                dve.tensor_scalar(c3[:, :, 0:E], s_next[:, :, :], 2.0 * WS, None, ALU.mult).then_inc(c_step, 1)
                dve.wait_ge(c_step, v + 1)
                dve.scalar_tensor_tensor(c3[:, :, 32:32 + E], s_next[:, :, :], 2.0 * WS, c3[:, :, 0:E],
                                         ALU.mult, ALU.subtract)
                dve.tensor_copy(c3[:, :, 64:64 + E], c3[:, :, 0:E]).then_inc(c_ready, 1)

            def split_w1(e):
                dve.wait_ge(w1_hi_done, e + 1)
                dve.scalar_tensor_tensor(w1_lo[:, e], w1_raw[:, e].rearrange("h (p c) -> h c p", c=FC), WS,
                                         w1_hi[:, e], ALU.mult, ALU.subtract).then_inc(w1_split, 1)

            def split_w2(e):
                dve.wait_ge(w2_hi_done, e + 1)
                dve.scalar_tensor_tensor(w2_lo[:, e].rearrange("p c h -> p (c h)"), w2_raw[:, e], WS,
                                         w2_hi[:, e].rearrange("p c h -> p (c h)"), ALU.mult, ALU.subtract)\
                    .then_inc(w2_split, 1)

            def split_b2():
                dve.wait_ge(b2_loaded, 6 * 16)
                dve.tensor_scalar(b2_hi[:, :], b2_raw[:, :], WS, None, ALU.mult).then_inc(b2_step, 1)
                dve.wait_ge(b2_step, 1)
                dve.tensor_copy(b2_st[0:64, :], b2_hi[0:64, :])
                dve.scalar_tensor_tensor(b2_st[64:96, :], b2_raw[64:96, :], WS, b2_hi[64:96, :],
                                         ALU.mult, ALU.subtract).then_inc(b2_ready, 1)

            def split_qk(u):
                dve.wait_ge(q32_ready, u)
                dve.tensor_copy(q_hi[:, :], q32[:, :])
                dve.tensor_copy(k_hi[:, WIN:], k32[:, :]).then_inc(q_hi_done, 1)
                dve.wait_ge(q_hi_done, u)
                dve.tensor_tensor(q_lo[:, :], q32[:, :], q_hi[:, :], ALU.subtract)
                dve.tensor_tensor(k_lo[:, WIN:], k32[:, :], k_hi[:, WIN:], ALU.subtract).then_inc(q_split, 1)

            def keep_values(u):
                dve.wait_ge(v_done, u)
                dve.scalar_tensor_tensor(v32[:, :, :], m[:, 2, 0:HS * KVD].rearrange("p (j c) -> p j c", c=KVD), 1 / WS,
                                         bv[:, :].unsqueeze(1).broadcast_to([P, HS, KVD]), ALU.mult, ALU.add)\
                    .then_inc(v32_done, 1)
                dve.wait_ge(v32_done, u)
                src = v32[:, :, :].rearrange("p j (g d) -> p j g d", d=HD)
                for par in range(2):
                    r = slice(par * KW, (par + 1) * KW)
                    op = dve.tensor_copy(v_hi[r, :, :, par, 0:HD], src[r])
                op.then_inc(v_hi_done, 1)
                dve.wait_ge(v_hi_done, u)
                for par in range(2):
                    r = slice(par * KW, (par + 1) * KW)
                    op = dve.tensor_tensor(v_lo[r, :, :, par, 0:HD], src[r], v_hi[r, :, :, par, 0:HD], ALU.subtract)
                op.then_inc(v_ready, 1)

            def softmax_max(u, hf):
                dve.wait_ge(s_ready, nth_half(u, hf))
                dve.tensor_reduce(mx[:, :], m[:, 0:2, :].rearrange("p g (s k) -> p (g s) k", k=KW), AX.X, ALU.max)\
                    .then_inc(mx_done, 1)
                dve.wait_ge(mx_done, nth_half(u, hf))
                dve.tensor_scalar(mxs[:, :], mx[:, :], sink[:, 0:1], None, ALU.max).then_inc(mxs_done, 1)

            def softmax_less_max(u, hf):
                dve.wait_ge(mxs_done, nth_half(u, hf))
                dve.tensor_tensor(pe_[:, 0:NS * KW].rearrange("p (s k) -> p s k", k=KW),
                                  m[:, 0:2, :].rearrange("p g (s k) -> p (g s) k", k=KW),
                                  mxs[:, :].unsqueeze(2).broadcast_to([P, NS, KW]), ALU.subtract)
                dve.tensor_scalar(pe_[:, NS * KW:], mxs[:, :], -1.0, sink[:, 0:1], ALU.mult, ALU.add)\
                    .then_inc(p_ready, 1)

            def probs_lo(u, hf):
                for g in range(G):
                    dve.wait_ge(pt_hi_done, nth_group(u, hf, g))
                    dve.tensor_tensor(pt_lo[:, g, :, :].rearrange("p j k -> p (j k)"), m[:, g, :],
                                      pt_hi[:, g, :, :].rearrange("p j k -> p (j k)"), ALU.subtract)\
                        .then_inc(pt_ready, 1)

            def outputs_norm(u, hf):
                n = nth_half(u, hf)
                pv = m[:, 0, 0:HS * G * VC].rearrange("p (j g a c) -> p j g a c", g=G, a=2, c=VC)
                dve.wait_ge(pv_done, n)
                dve.tensor_tensor(den[:, :, :, :], pv[:, :, :, :, HD],
                                  pe_[:, NS * KW:].rearrange("p (g j a) -> p j g a", a=2, g=G), ALU.add)\
                    .then_inc(den_done, 1)
                dve.wait_ge(den_done, n)
                dve.reciprocal(rden[:, :, :, :], den[:, :, :, :]).then_inc(rden_done, 1)
                dve.wait_ge(rden_done, n)
                for par in range(2):
                    op = dve.tensor_tensor(o32[:, par::2, :, :], pv[:, :, :, par, 0:HD],
                                           rden[:, :, :, par].unsqueeze(3).broadcast_to([P, HS // 2, G, HD]), ALU.mult)
                op.then_inc(o_done, 1)

            def outputs_turn(u, hf):
                n = nth_half(u, hf)
                cols = slice(hf * HS * WIN, (hf + 1) * HS * WIN)
                dve.wait_ge(o_done, n)
                dve.transpose(ot32[:, :], o32[:, :, :, :].rearrange("p s g d -> p (s g d)")).then_inc(ot_turned, 1)
                dve.wait_ge(ot_turned, n)
                dve.tensor_copy(ot_hi[:, cols], ot32[:, :]).then_inc(ot_hi_done, 1)
                dve.wait_ge(ot_hi_done, n)
                dve.tensor_tensor(ot_lo[:, cols], ot32[:, :], ot_hi[:, cols], ALU.subtract).then_inc(ot_ready, 1)

            def unit(u, halves=(), first=False, last=False):
                at = DVE_AT0 if first else DVE_AT
                for s in range(NE):
                    for q in range(FC):
                        i = FC * s + q
                        if 0 in halves and i == at["stats_att"]:
                            dve.wait_ge(y_used, u * NE)
                        if 0 in halves and i == at["var_att"]:
                            dve.wait_ge(att.s_stats, u)
                        if not last and i == at["var_pre"]:
                            dve.wait_ge(pre.s_stats, u + 2)
                        hidden(u, s, q)
                        if 0 in halves and i == at["var_att"]:
                            variances(att, u)
                        if not last and i == at["var_pre"]:
                            variances(pre, u + 2)
                        if q == 0:
                            if s >= 2:
                                combine(u, s - 2)
                            elif not first:
                                combine(u - 1, NE - 2 + s)
                        if 0 in halves:
                            if i == at["stats_att"]:
                                statistics(att, u, slot(x, u - 1))
                            if i == at["xn_att"]:
                                normalize(att, u, slot(x, u - 1))
                            if i == at["lo_att"]:
                                normed_lo(att, u, xa_lo[:, WIN:], xa_hi[:, WIN:], 2)
                            if i == at["split_qk"]:
                                split_qk(u)
                            if i == at["v"]:
                                keep_values(u)
                        for hf in halves:
                            if i == at["max"][hf]:
                                softmax_max(u, hf)
                            if i == at["less"][hf]:
                                softmax_less_max(u, hf)
                            if i == at["pt_lo"][hf]:
                                probs_lo(u, hf)
                            if i == at["norm"][hf]:
                                outputs_norm(u, hf)
                            if i == at["turn_o"][hf]:
                                outputs_turn(u, hf)
                        if 1 in halves and i == at["xres"]:
                            dve.wait_ge(y_used, (u - 1) * NE)
                            dve.tensor_tensor(xres[:, :, :], slot(x, u - 2),
                                              bo[:, :].unsqueeze(1).broadcast_to([P, TT, D]), ALU.add)\
                                .then_inc(xres_done, 1)
                        if 1 in halves and i == at["add"]:
                            dve.wait_ge(xres_done, u - 1)
                            dve.wait_ge(out_ready, u - 1)
                            dve.scalar_tensor_tensor(slot(x, u + NBLK - 2), m[:, 2, :].rearrange("p (t d) -> p t d", d=D),
                                                     1 / WS, xres[:, :, :], ALU.mult, ALU.add).then_inc(x_attended, 1)
                        if not last:
                            if i == at["stats_pre"]:
                                if first:
                                    dve.wait_ge(x_loaded[1], 16)
                                elif isinstance(u, int) and u == 1:
                                    for b in range(2, NBLK):
                                        dve.wait_ge(x_loaded[b], 16)
                                statistics(pre, u + 2, slot(x, u + 1))
                            if i == at["xn_pre"]:
                                normalize(pre, u + 2, slot(x, u + 1))
                            if i == at["lo_pre"]:
                                normed_lo(pre, u + 2, slot(xt_lo, u + 1), slot(xt_hi, u + 1), 2)
                            for step in range(STEPS):
                                if i == at["router"] + step + (step == STEPS - 1):
                                    router(u + 1, step)
                        if first:
                            for step in range(STEPS):
                                if i == at["router0"] + (step > 3) + (step == STEPS - 1):
                                    router(0, step)
                        if i == at["s_cur"]:
                            wait(dve, y_used, u * NE)
                            dve.wait_ge(gate_step, (u + 1) * STEPS)
                            dve.tensor_copy(s_cur[:, :, :], s_next[:, :, :]).then_inc(s_cur_ready, 1)
                        if i == at["c"]:
                            weights_c(u)
                        if first:
                            if q == at["w1"] and s < NE - 2:
                                split_w1(s + 2)
                            if q == at["w2"] and s < NE - 1:
                                split_w2(s + 1)
                            if i == at["b2"]:
                                split_b2()
                            if i == at["wo"]:
                                dve.wait_ge(aw_loaded, 16 * AW_LOADS)
                                dve.tensor_copy(wo_perm[:, :].rearrange("p (h g d) -> p h g d", h=HG, g=G),
                                                wo_raw[:, :].rearrange("p (g h d) -> p h g d", h=HG, g=G))\
                                    .then_inc(wo_ready, 1)
                            if i == at["w_lo"]:
                                dve.wait_ge(aw_hi_done, 1)
                                dve.scalar_tensor_tensor(aw_lo[:, :], m[:, 0, 0:AW], WS, aw_hi[:, :], ALU.mult,
                                                         ALU.subtract).then_inc(aw_ready, 1)

            dve.memset(zero[:, :], 0.0)
            dve.memset(b2_raw[:, :], 0.0).then_inc(b2_zero, 1)
            dve.memset(c3[:, :, :], 0.0).then_inc(dve_made, 1)
            dve.wait_ge(dve_made, 1)
            dve.memset(c3[:, :, E:E + 1], 1.0)
            dve.memset(c3[:, :, 64 + E:65 + E], 1.0)
            dve.memset(xa_hi[:, 0:WIN], 0.0)
            dve.memset(xa_lo[:, 0:WIN], 0.0)
            dve.memset(k_hi[:, 0:WIN], 0.0)
            dve.memset(k_lo[:, 0:WIN], 0.0)
            dve.memset(v_lo[:, :, :, :, :], 0.0)
            dve.memset(v_hi[:, :, :, :, :], 0.0).then_inc(dve_made, 1)
            dve.wait_ge(dve_made, 2)
            for par in range(2):
                dve.memset(v_hi[par * KW:(par + 1) * KW, :, :, par, HD:HD + 1], 1.0)
            dve.wait_ge(x_loaded[0], 16)
            statistics(pre, 1, slot(x, 0))
            dve.wait_ge(pre.s_stats, 1)
            variances(pre, 1)
            dve.wait_ge(made, 3)
            dve.tensor_copy(ident16[:, :], ident[:, :])
            dve.tensor_copy(identb[:, :], ident[:, :])
            normalize(pre, 1, slot(x, 0))
            split_w1(0)
            dve.wait_ge(gate_hi_done, 1)
            dve.scalar_tensor_tensor(gate_lo[:, :], m[:, 1, 0:E], WS, gate_hi[:, :], ALU.mult, ALU.subtract)\
                .then_inc(gate_ready, 1)
            normed_lo(pre, 1, slot(xt_lo, 0), slot(xt_hi, 0), 2)
            split_w1(1)
            split_w2(0)
            dve.wait_ge(made, 6)
            unit(0, first=True)
            dve.wait_ge(made, 21)
            unit(1, halves=(0,))
            with dve.Fori(2, NBLK + 1) as u:
                unit(u, halves=(0, 1))
            unit(NBLK + 1, halves=(1,))
            unit(NBLK + 2)
            unit(NU - 1, last=True)
            combine(NU - 1, NE - 2)
            combine(NU - 1, NE - 1, final=True)


_INS = ["L0_attn_x", "L0_attn_sink_bias", "L0_attn_Wq", "L0_attn_bq", "L0_attn_Wk", "L0_attn_bk", "L0_attn_Wv",
        "L0_attn_bv", "L0_attn_Wo", "L0_attn_bo", "L0_ffn_gate_w", "L0_ffn_W1", "L0_ffn_b1", "L0_ffn_W2",
        "L0_ffn_b2", "L0_ffn_sW1", "L0_ffn_sb1", "L0_ffn_sW2", "L0_ffn_sb2"]
_OUTS = [((4, 512, 128), "float32")]


def kernel(**inputs):
    import numpy as _np
    import concourse.bacc as _bacc
    from concourse import mybir as _mybir
    from concourse.bass_utils import run_bass_kernel_spmd as _run

    nc = _bacc.Bacc("TRN2", target_bir_lowering=False, num_devices=1)
    arrays, args = {}, []
    for name in _INS:
        a = _np.ascontiguousarray(inputs[name])
        arrays[f"in_{name}_dram"] = a
        args.append(nc.dram_tensor(f"in_{name}_dram", a.shape, _mybir.dt.from_np(a.dtype), kind="ExternalInput").ap())
    for i, (shape, dtype) in enumerate(_OUTS):
        dt = _mybir.dt.from_np(_np.dtype(dtype))
        args.append(nc.dram_tensor(f"out_{i}_dram", shape, dt, kind="ExternalOutput").ap())
    macaron_kernel(nc, *args)
    r = _run(nc, [arrays], core_ids=[0])
    return r.results[0]["out_0_dram"]
```
